# Optimizing a Trainium2 kernel written in Bass

```python
import numpy as np
import jax
import jax.numpy as jnp

def _softmax(x, axis=-1):
    return jax.nn.softmax(x, axis=axis)

def _gelu(x):
    return jax.nn.gelu(x, approximate=True)

def _silu(x):
    return jax.nn.silu(x)

def _sigmoid(x):
    return jax.nn.sigmoid(x)

def _layernorm(x, axis=-1, eps=1e-05):
    m = jnp.mean(x, axis=axis, keepdims=True)
    v = jnp.var(x, axis=axis, keepdims=True)
    return (x - m) / jnp.sqrt(v + eps)

def _scatter_add(tgt, idx, src, axis=0):
    return tgt.at[idx].add(src)

def _segment_sum(src, seg, n):
    return jax.ops.segment_sum(src, seg, n)
kernel_name = 'mk_decoder_preln_d1_seqx_r4_204617'

def setup_inputs(seed: int=0):
    np.random.seed(seed)
    _w = jnp.asarray

    def _rec_inputs():
        import jax
        import jax.numpy as jnp
        _rk = jax.random.key(seed)
        x = -0.0003929 + 0.9999 * jax.random.normal(jax.random.fold_in(_rk, 1), (16, 256, 512), jnp.float32)
        _lenS = 256 - jax.random.randint(jax.random.fold_in(_rk, 7), (16,), 0, max(1, 256 // 4) + 1, jnp.int32)
        _lenS2 = 256 - jax.random.randint(jax.random.fold_in(_rk, 8), (16,), 0, max(1, 256 // 4) + 1, jnp.int32)
        _ctx_2048P = jax.random.normal(jax.random.fold_in(_rk, 11), (16, 16, 512), jnp.float32)
        _ctx_2048c = jax.random.dirichlet(jax.random.fold_in(_rk, 511), 0.3 * jnp.ones((16,), jnp.float32), (16, 256))
        _ctx_2048t = jnp.einsum('bsk,bkd->bsd', _ctx_2048c, _ctx_2048P)
        _ctx_2048t = _ctx_2048t * jax.lax.rsqrt(jnp.mean(jnp.square(_ctx_2048t)) + 1e-12) * 0.953939
        ctx_2048 = 2.81802e-05 + 1.00001 * (_ctx_2048t + 0.3 * jax.random.normal(jax.random.fold_in(_rk, 611), (16, 256, 512), jnp.float32))
        return (x, ctx_2048)
    x, ctx_2048 = _rec_inputs()

    def _L0_attn_setup():
        import jax, jax.numpy as jnp
        import numpy as np
        import math
        D = 512
        H = 16
        KV = 4
        DH = D // H
        REP = H // KV
        LAMBDA_INIT = 0.8 - 0.6 * math.exp(-0.3 * 0)
        ROPE_BASE = 10000.0
        EPS = 1e-05

        def _rope(x, cos, sin):
            x1, x2 = (x[..., ::2], x[..., 1::2])
            c = cos[None, None]
            s = sin[None, None]
            o1 = x1 * c - x2 * s
            o2 = x1 * s + x2 * c
            return jnp.stack([o1, o2], axis=-1).reshape(x.shape)

        def _forward(x, Wq, Wk, Wv, Wo, lambda_q1, lambda_k1, lambda_q2, lambda_k2, gn_w, gn_b):
            B, T, _ = x.shape
            q = (x @ Wq).reshape(B, T, H, 2 * DH).transpose(0, 2, 1, 3)
            k = (x @ Wk).reshape(B, T, KV, 2 * DH).transpose(0, 2, 1, 3)
            v = (x @ Wv).reshape(B, T, KV, 2 * DH).transpose(0, 2, 1, 3)
            q1, q2 = (q[..., :DH], q[..., DH:])
            k1, k2 = (k[..., :DH], k[..., DH:])
            inv = 1.0 / ROPE_BASE ** (jnp.arange(0, DH, 2, dtype=jnp.float32) / DH)
            freqs = jnp.arange(T, dtype=jnp.float32)[:, None] * inv[None, :]
            cos, sin = (jnp.cos(freqs), jnp.sin(freqs))
            q1, q2 = (_rope(q1, cos, sin), _rope(q2, cos, sin))
            k1, k2 = (_rope(k1, cos, sin), _rope(k2, cos, sin))
            k1 = jnp.repeat(k1, REP, axis=1)
            k2 = jnp.repeat(k2, REP, axis=1)
            v = jnp.repeat(v, REP, axis=1)
            mask = jnp.triu(jnp.full((T, T), -jnp.inf, dtype=x.dtype), k=1)[None, None]
            scale = 1.0 / math.sqrt(DH)
            s1 = jnp.einsum('bhtd,bhsd->bhts', q1, k1) * scale + mask
            s2 = jnp.einsum('bhtd,bhsd->bhts', q2, k2) * scale + mask
            a1 = jax.nn.softmax(s1, axis=-1)
            a2 = jax.nn.softmax(s2, axis=-1)
            lam = jnp.exp(jnp.sum(lambda_q1 * lambda_k1)) - jnp.exp(jnp.sum(lambda_q2 * lambda_k2)) + LAMBDA_INIT
            diff = a1 - lam * a2
            out = jnp.einsum('bhts,bhsd->bhtd', diff, v)
            out = out.transpose(0, 2, 1, 3)
            mean = jnp.mean(out, axis=(1, 3), keepdims=True)
            var = jnp.var(out, axis=(1, 3), keepdims=True)
            out = (out - mean) * jax.lax.rsqrt(var + EPS)
            out = out * gn_w.reshape(1, 1, H, 2 * DH) + gn_b.reshape(1, 1, H, 2 * DH)
            out = out.reshape(B, T, 2 * H * DH) * (1.0 - LAMBDA_INIT)
            return out @ Wo
        key = jax.random.key(seed)
        ks = jax.random.split(key, 12)
        B, T = (1, 512)
        s = 0.02
        return {'x': jax.random.normal(ks[0], (B, T, D), jnp.float32), 'Wq': jax.random.normal(ks[1], (D, 2 * H * DH), jnp.float32) * s, 'Wk': jax.random.normal(ks[2], (D, 2 * KV * DH), jnp.float32) * s, 'Wv': jax.random.normal(ks[3], (D, 2 * KV * DH), jnp.float32) * s, 'Wo': jax.random.normal(ks[4], (2 * H * DH, D), jnp.float32) * s, 'lambda_q1': jax.random.normal(ks[5], (DH,), jnp.float32) * 0.1, 'lambda_k1': jax.random.normal(ks[6], (DH,), jnp.float32) * 0.1, 'lambda_q2': jax.random.normal(ks[7], (DH,), jnp.float32) * 0.1, 'lambda_k2': jax.random.normal(ks[8], (DH,), jnp.float32) * 0.1, 'gn_w': jnp.ones((2 * H * DH,), jnp.float32), 'gn_b': jnp.zeros((2 * H * DH,), jnp.float32)}
    _L0_attn_all = _L0_attn_setup()
    _L0_attn_in = {k: v for k, v in _L0_attn_all.items() if k in ('Wq', 'Wk', 'Wv', 'Wo', 'lambda_q1', 'lambda_k1', 'lambda_q2', 'lambda_k2', 'gn_w', 'gn_b')}
    del _L0_attn_all

    def _L0_xattn_setup():
        import jax, jax.numpy as jnp
        import numpy as np
        N, D, L = (8, 256, 512)
        key = jax.random.key(seed)
        ks = jax.random.split(key, 5)
        s = 1.0 / np.sqrt(D)
        return {'X1': jax.random.normal(ks[0], (N, D, L), dtype=jnp.float32), 'X2': jax.random.normal(ks[1], (N, D, L), dtype=jnp.float32), 'QW': jax.random.normal(ks[2], (D, D), dtype=jnp.float32) * s, 'Qb': jnp.zeros((D,), dtype=jnp.float32), 'KW': jax.random.normal(ks[3], (D, D), dtype=jnp.float32) * s, 'Kb': jnp.zeros((D,), dtype=jnp.float32), 'VW': jax.random.normal(ks[4], (D, D), dtype=jnp.float32) * s, 'Vb': jnp.zeros((D,), dtype=jnp.float32)}
    _L0_xattn_all = _L0_xattn_setup()
    _L0_xattn_in = {k: v for k, v in _L0_xattn_all.items() if k in ('QW', 'Qb', 'KW', 'Kb', 'VW', 'Vb')}
    del _L0_xattn_all

    def _L0_ffn_setup():
        import jax, jax.numpy as jnp
        import numpy as np
        B, S, D = (1, 256, 512)
        E, K, F = (64, 8, 192)
        C = 64

        def _moe(x, router_w, w1, v1, w2):
            T = x.shape[0]
            logits = x @ router_w.T
            probs = jax.nn.softmax(logits, axis=-1)
            wts, idx = jax.lax.top_k(probs, K)
            wts = wts / jnp.sum(wts, axis=-1, keepdims=True)
            R = T * K
            e_flat = idx.reshape(-1)
            tok = jnp.arange(R) // K
            order = jnp.argsort(e_flat)
            e_s, tok_s = (e_flat[order], tok[order])
            w_s = wts.reshape(-1)[order]
            counts = jnp.bincount(e_flat, length=E)
            starts = jnp.cumsum(counts) - counts
            pos = jnp.arange(R) - starts[e_s]
            valid = pos < C
            pos_c = jnp.minimum(pos, C - 1)
            xg = jnp.zeros((E, C, D), x.dtype).at[e_s, pos_c].add(jnp.where(valid[:, None], x[tok_s], 0.0))
            h = jax.nn.silu(jnp.einsum('ecd,efd->ecf', xg, w1)) * jnp.einsum('ecd,efd->ecf', xg, v1)
            y = jnp.einsum('ecf,efd->ecd', h, w2)
            yr = y[e_s, pos_c] * jnp.where(valid, w_s, 0.0)[:, None]
            return jnp.zeros((T, D), x.dtype).at[tok_s].add(yr)
        key = jax.random.key(seed)
        k0, k1, k2, k3, k4 = jax.random.split(key, 5)
        return {'hidden_states': jax.random.normal(k0, (B, S, D), jnp.float32), 'router_w': jax.random.normal(k1, (E, D), jnp.float32) * 0.02, 'w1': jax.random.normal(k2, (E, F, D), jnp.float32) * 0.02, 'v1': jax.random.normal(k3, (E, F, D), jnp.float32) * 0.02, 'w2': jax.random.normal(k4, (E, F, D), jnp.float32) * 0.02}
    _L0_ffn_all = _L0_ffn_setup()
    _L0_ffn_in = {k: v for k, v in _L0_ffn_all.items() if k in ('router_w', 'w1', 'v1', 'w2')}
    del _L0_ffn_all
    return {'x': x, 'ctx_2048': ctx_2048, 'L0_attn_Wq': _L0_attn_in['Wq'], 'L0_attn_Wk': _L0_attn_in['Wk'], 'L0_attn_Wv': _L0_attn_in['Wv'], 'L0_attn_Wo': _L0_attn_in['Wo'], 'L0_attn_lambda_q1': _L0_attn_in['lambda_q1'], 'L0_attn_lambda_k1': _L0_attn_in['lambda_k1'], 'L0_attn_lambda_q2': _L0_attn_in['lambda_q2'], 'L0_attn_lambda_k2': _L0_attn_in['lambda_k2'], 'L0_attn_gn_w': _L0_attn_in['gn_w'], 'L0_attn_gn_b': _L0_attn_in['gn_b'], 'L0_xattn_QW': _L0_xattn_in['QW'], 'L0_xattn_Qb': _L0_xattn_in['Qb'], 'L0_xattn_KW': _L0_xattn_in['KW'], 'L0_xattn_Kb': _L0_xattn_in['Kb'], 'L0_xattn_VW': _L0_xattn_in['VW'], 'L0_xattn_Vb': _L0_xattn_in['Vb'], 'L0_ffn_router_w': _L0_ffn_in['router_w'], 'L0_ffn_w1': _L0_ffn_in['w1'], 'L0_ffn_v1': _L0_ffn_in['v1'], 'L0_ffn_w2': _L0_ffn_in['w2']}

def reference(x, ctx_2048, L0_attn_Wq, L0_attn_Wk, L0_attn_Wv, L0_attn_Wo, L0_attn_lambda_q1, L0_attn_lambda_k1, L0_attn_lambda_q2, L0_attn_lambda_k2, L0_attn_gn_w, L0_attn_gn_b, L0_xattn_QW, L0_xattn_Qb, L0_xattn_KW, L0_xattn_Kb, L0_xattn_VW, L0_xattn_Vb, L0_ffn_router_w, L0_ffn_w1, L0_ffn_v1, L0_ffn_w2):
    import jax
    import jax.numpy as jnp

    def _L0_attn_ref(x, Wq, Wk, Wv, Wo, lambda_q1, lambda_k1, lambda_q2, lambda_k2, gn_w, gn_b):
        import jax, jax.numpy as jnp
        import numpy as np
        import math
        D = 512
        H = 16
        KV = 4
        DH = D // H
        REP = H // KV
        LAMBDA_INIT = 0.8 - 0.6 * math.exp(-0.3 * 0)
        ROPE_BASE = 10000.0
        EPS = 1e-05

        def _rope(x, cos, sin):
            x1, x2 = (x[..., ::2], x[..., 1::2])
            c = cos[None, None]
            s = sin[None, None]
            o1 = x1 * c - x2 * s
            o2 = x1 * s + x2 * c
            return jnp.stack([o1, o2], axis=-1).reshape(x.shape)

        def _forward(x, Wq, Wk, Wv, Wo, lambda_q1, lambda_k1, lambda_q2, lambda_k2, gn_w, gn_b):
            B, T, _ = x.shape
            q = (x @ Wq).reshape(B, T, H, 2 * DH).transpose(0, 2, 1, 3)
            k = (x @ Wk).reshape(B, T, KV, 2 * DH).transpose(0, 2, 1, 3)
            v = (x @ Wv).reshape(B, T, KV, 2 * DH).transpose(0, 2, 1, 3)
            q1, q2 = (q[..., :DH], q[..., DH:])
            k1, k2 = (k[..., :DH], k[..., DH:])
            inv = 1.0 / ROPE_BASE ** (jnp.arange(0, DH, 2, dtype=jnp.float32) / DH)
            freqs = jnp.arange(T, dtype=jnp.float32)[:, None] * inv[None, :]
            cos, sin = (jnp.cos(freqs), jnp.sin(freqs))
            q1, q2 = (_rope(q1, cos, sin), _rope(q2, cos, sin))
            k1, k2 = (_rope(k1, cos, sin), _rope(k2, cos, sin))
            k1 = jnp.repeat(k1, REP, axis=1)
            k2 = jnp.repeat(k2, REP, axis=1)
            v = jnp.repeat(v, REP, axis=1)
            mask = jnp.triu(jnp.full((T, T), -jnp.inf, dtype=x.dtype), k=1)[None, None]
            scale = 1.0 / math.sqrt(DH)
            s1 = jnp.einsum('bhtd,bhsd->bhts', q1, k1) * scale + mask
            s2 = jnp.einsum('bhtd,bhsd->bhts', q2, k2) * scale + mask
            a1 = jax.nn.softmax(s1, axis=-1)
            a2 = jax.nn.softmax(s2, axis=-1)
            lam = jnp.exp(jnp.sum(lambda_q1 * lambda_k1)) - jnp.exp(jnp.sum(lambda_q2 * lambda_k2)) + LAMBDA_INIT
            diff = a1 - lam * a2
            out = jnp.einsum('bhts,bhsd->bhtd', diff, v)
            out = out.transpose(0, 2, 1, 3)
            mean = jnp.mean(out, axis=(1, 3), keepdims=True)
            var = jnp.var(out, axis=(1, 3), keepdims=True)
            out = (out - mean) * jax.lax.rsqrt(var + EPS)
            out = out * gn_w.reshape(1, 1, H, 2 * DH) + gn_b.reshape(1, 1, H, 2 * DH)
            out = out.reshape(B, T, 2 * H * DH) * (1.0 - LAMBDA_INIT)
            return out @ Wo
        return _forward(x, Wq, Wk, Wv, Wo, lambda_q1, lambda_k1, lambda_q2, lambda_k2, gn_w, gn_b)

    def _L0_xattn_ref(X1, X2, QW, Qb, KW, Kb, VW, Vb):
        import jax, jax.numpy as jnp
        import numpy as np
        N, D, L = (8, 256, 512)
        q = jnp.einsum('ndl,ed->nle', X1, QW) + Qb
        k = jnp.einsum('ndl,ed->nle', X2, KW) + Kb
        v = jnp.einsum('ndl,ed->nle', X2, VW) + Vb
        scores = jnp.einsum('nqd,nkd->nqk', q, k)
        attn = jax.nn.softmax(scores, axis=-1)
        H = jnp.einsum('nqk,nkd->nqd', attn, v)
        return jnp.swapaxes(H, -1, -2)

    def _L0_ffn_ref(hidden_states, router_w, w1, v1, w2):
        import jax, jax.numpy as jnp
        import numpy as np
        B, S, D = (1, 256, 512)
        E, K, F = (64, 8, 192)
        C = 64

        def _moe(x, router_w, w1, v1, w2):
            T = x.shape[0]
            logits = x @ router_w.T
            probs = jax.nn.softmax(logits, axis=-1)
            wts, idx = jax.lax.top_k(probs, K)
            wts = wts / jnp.sum(wts, axis=-1, keepdims=True)
            R = T * K
            e_flat = idx.reshape(-1)
            tok = jnp.arange(R) // K
            order = jnp.argsort(e_flat)
            e_s, tok_s = (e_flat[order], tok[order])
            w_s = wts.reshape(-1)[order]
            counts = jnp.bincount(e_flat, length=E)
            starts = jnp.cumsum(counts) - counts
            pos = jnp.arange(R) - starts[e_s]
            valid = pos < C
            pos_c = jnp.minimum(pos, C - 1)
            xg = jnp.zeros((E, C, D), x.dtype).at[e_s, pos_c].add(jnp.where(valid[:, None], x[tok_s], 0.0))
            h = jax.nn.silu(jnp.einsum('ecd,efd->ecf', xg, w1)) * jnp.einsum('ecd,efd->ecf', xg, v1)
            y = jnp.einsum('ecf,efd->ecd', h, w2)
            yr = y[e_s, pos_c] * jnp.where(valid, w_s, 0.0)[:, None]
            return jnp.zeros((T, D), x.dtype).at[tok_s].add(yr)
        b, s, d = hidden_states.shape
        x = hidden_states.transpose(1, 0, 2).reshape(s * b, d)
        out = _moe(x, router_w, w1, v1, w2)
        return out.reshape(s, b, d).transpose(1, 0, 2)
    x = x + _L0_attn_ref(_layernorm(x, axis=-1), L0_attn_Wq, L0_attn_Wk, L0_attn_Wv, L0_attn_Wo, L0_attn_lambda_q1, L0_attn_lambda_k1, L0_attn_lambda_q2, L0_attn_lambda_k2, L0_attn_gn_w, L0_attn_gn_b)
    x = x + _L0_xattn_ref(_layernorm(x, axis=-1), ctx_2048, L0_xattn_QW, L0_xattn_Qb, L0_xattn_KW, L0_xattn_Kb, L0_xattn_VW, L0_xattn_Vb)
    x = x + _L0_ffn_ref(_layernorm(x, axis=-1), L0_ffn_router_w, L0_ffn_w1, L0_ffn_v1, L0_ffn_w2)
    return x

_drawn_inputs = setup_inputs


def setup_inputs(seed=0):
    import zlib

    import numpy as np

    out = dict(_drawn_inputs(seed))
    spreads = {'L0_attn_gn_w': (1.0, 0.2),
     'L0_attn_gn_b': (0.0, 0.1),
     'L0_xattn_Qb': (0.0, 0.1),
     'L0_xattn_Kb': (0.0, 2.0),
     'L0_xattn_Vb': (0.0, 0.405)}
    factors = {'L0_attn_lambda_k1': 5.907,
     'L0_attn_lambda_q2': 8.0,
     'L0_attn_lambda_k2': 8.0,
     'L0_ffn_router_w': 8.0,
     'L0_ffn_w1': 8.0,
     'L0_ffn_v1': 8.0,
     'L0_ffn_w2': 8.0}
    for name, (base, spread) in spreads.items():
        noise = np.random.default_rng([zlib.crc32(name.encode()), seed]).standard_normal(out[name].shape)
        drawn = base * np.exp(spread * noise) if base else spread * noise
        out[name] = jnp.asarray(drawn.astype(out[name].dtype))
    for name, factor in factors.items():
        out[name] = (out[name] * factor).astype(out[name].dtype)
    return out
```

```python
import math
from contextlib import ExitStack

import numpy as np

import concourse.bass as bass
from concourse import mybir

FP32 = mybir.dt.float32
BF16 = mybir.dt.bfloat16
I32 = mybir.dt.int32
ALU = mybir.AluOpType
ACT = mybir.ActivationFunctionType
AX = mybir.AxisListType

P = 128
B, T, D = 16, 256, 512
H, KV, DH = 16, 4, 32
TT = T // P
KC = D // P
HD = 2 * DH
UNITS = H // 2
NQK = 2 * H * DH + 2 * KV * DH
NQKV = NQK + KV * HD
ROPE_PARTS = [(0, 512), (512, 512), (1024, 256)]
BANK = 512
EXPERTS, TOPK, FF, CAP = 64, 8, 192, 64
TOKENS = B * T
ROW = D + EXPERTS
PAIRS = EXPERTS // 2
LAMBDA_INIT = 0.8 - 0.6 * math.exp(0.0)
EPS = 1e-5
SCALE = 1.0 / math.sqrt(DH)
MASKED = -1e30
DVE_STEPS = 49

IDENT, TRI, HEADS, COS, SIN, KEY0, SPARE, TAB = 0, 128, 640, 768, 832, 896, 898, 962
GW, GB, QB, KB, VB, LAM, COLS = 0, 8, 16, 18, 20, 22, 150


class Ring:

    def __init__(self, first, banks, names):
        assert len(names) % banks == 0
        self.per = len(names) // banks
        self.at = {name: (first + n % banks, n // banks) for n, name in enumerate(names)}

    def __getitem__(self, name):
        return self.at[name]


def sums():
    names = [f"{what}{t}" for t in range(TT) for what in ("qa", "qb", "kv")] + ["kx0", "kx1"]
    for s in range(2, UNITS + 3):
        names += [f"pv{s - 2}"] * (s < UNITS + 2) + [f"oT{s - 3}"] * (s >= 3)
    return names + ["vx0", "vx1", "gmean", "gvar", "wo0", "wo1", "qx0", "qx1", "h0", "h1", "route0", "route1"]


SCORE_BANKS = Ring(0, 4, [f"s{j}{part}" for j in range(UNITS) for part in "ABC"] + [f"x{q}" for q in range(4)])
TURN_BANKS = Ring(4, 2, ["xnT0", "xnT1", "kT", "qT0", "qT1", "qT2", "qT3"]
                  + [f"dT{j}{h}" for j in range(UNITS) for h in range(2)]
                  + ["pT0", "pT1", "pT2", "pT3", "rT0", "rT1", "keyT"])
SUM_BANKS = Ring(6, 2, sums())

def build(nc, x, ctx, wqkv, wo, wx, wr, cols, tabs, w13, w2, out, table):
    with ExitStack() as stack:
        psum = stack.enter_context(nc.psum_tensor("psum", [P, 8, BANK], FP32))
        keys = stack.enter_context(nc.sbuf_tensor("keys", [P, B * P], FP32))
        tab = stack.enter_context(nc.sbuf_tensor("tab", [P, TAB], FP32))
        with ExitStack() as st:
            attention(nc, st, psum, x, ctx, wqkv, wo, wx, wr, cols, tabs, out, table, keys, tab)
        with ExitStack() as st:
            experts(nc, st, psum, w13, w2, out, table, keys, tab)


def alone(eng):
    eng.nop(nofuse=True)


def attention(nc, st, psum, x, ctx, wqkv, wo, wx, wr, cols, tabs, out, table, keys, tab):
    def sb(name, shape, dt=FP32):
        return st.enter_context(nc.sbuf_tensor(name, shape, dt))

    def sem(name):
        return st.enter_context(nc.semaphore(name))

    wqkv_sb = sb("wqkv_sb", [P, KC, NQKV])
    wo_sb = sb("wo_sb", [P, UNITS, D])
    wx_sb = sb("wx_sb", [P, 3, TT, T])
    wr_sb = sb("wr_sb", [P, KC, EXPERTS])
    col = sb("col", [P, COLS])
    ident = tab[:, IDENT:IDENT + P]
    ident_b = sb("ident_b", [P, P], BF16)
    tri_b = sb("tri_b", [P, 4, P], BF16)
    gnw, gnb = sb("gnw", [P, UNITS]), sb("gnb", [P, UNITS])
    half = sb("half", [P, UNITS])
    prod, dots, lam, neglam = sb("prod", [P, 2, DH]), sb("dots", [P, 2]), sb("lam", [P, 2]), sb("neglam", [P, 1])
    keycol = sb("keycol", [P, TT])

    xt, ct, xn = sb("xt", [P, TT, D]), sb("ct", [P, TT, D]), sb("xn", [P, TT, D])
    xnT = sb("xnT", [P, KC, T])
    rope1, rope2 = sb("rope1", [P, 2, BANK]), sb("rope2", [P, 2, BANK])
    qk = sb("qk", [P, TT, NQK])
    qT = sb("qT", [P, UNITS, T])
    kz = sb("kz", [P, 2, 4, T])
    v = sb("v", [P, TT, KV * HD])
    ex = sb("ex", [P, 2, 4, 3 * P])
    diff = sb("diff", [P, 2, 2, 3 * P])
    diffT = sb("diffT", [P, 2, 2, 3 * P])
    osc = sb("osc", [P, 2, TT, P])
    oT = sb("oT", [P, UNITS, T])
    x1 = sb("x1", [P, TT, D])
    qx, kx, vx = sb("qx", [P, 2, D]), sb("kx", [P, 2, D]), sb("vx", [P, 4, T])
    pr, prT = sb("pr", [P, 4, D]), sb("prT", [P, 4, D])
    row = sb("row", [P, TT, ROW])
    rT = sb("rT", [P, KC, T])
    st6, mv, ve, rstd = sb("st6", [P, TT, 6]), sb("mv", [P, TT, 2]), sb("ve", [P, TT]), sb("rstd", [P, TT])
    mx, nm, den, rden = (sb(n, [P, 2, 8]) for n in ("mx", "nm", "den", "rden"))
    cmul = sb("cmul", [P, 2, 4])
    go6, gmv = sb("go6", [P, UNITS, 6]), sb("gmv", [P, UNITS, 2])
    gm, gdev, gsq, gve, grs, ga, gb = (sb(n, [P, UNITS]) for n in ("gm", "gdev", "gsq", "gve", "grs", "ga", "gb"))
    mxx, nmx, denx, rdenx = (sb(n, [P, 4]) for n in ("mxx", "nmx", "denx", "rdenx"))
    rmx, rnm, rden1, rr, s8, r8 = (sb(n, [P, TT]) for n in ("rmx", "rnm", "rden1", "rr", "s8", "r8"))
    prob, rest, chosen, pexp, keyed = (sb(n, [P, TT, EXPERTS]) for n in ("prob", "rest", "chosen", "pexp", "keyed"))
    top = sb("top", [P, TT, TOPK])

    loaded = sem("loaded")
    made = sem("made")
    zeroed = sem("zeroed")
    lam_exp = sem("lam_exp")
    x_in, ctx_in = sem("x_in"), sem("ctx_in")
    full = [sem(f"bank{n}_full") for n in range(8)]
    free = [sem(f"bank{n}_free") for n in range(8)]
    stats, ve_in, rooted = sem("stats"), sem("ve_in"), sem("rooted")
    normed = sem("normed")
    k_roped, rope_sum = sem("k_roped"), sem("rope_sum")
    max_in, diff_in = sem("max_in"), sem("diff_in")
    gstat, groot, gdone = sem("gstat"), sem("groot"), sem("gdone")
    xmax, xrec, xnorm = sem("xmax"), sem("xrec"), sem("xnorm")
    row_in, rmax_in = sem("row_in"), sem("rmax_in")
    out_done, row_done = sem("out_done"), sem("row_done")
    step = sem("step")

    def begin(eng, ring, i, name):
        bank, turn = ring[name]
        eng.wait_ge(free[bank], i * ring.per + (turn + 1))
        return psum[:, bank, :], full[bank]

    def filled(eng, ring, i, name):
        bank, turn = ring[name]
        eng.wait_ge(full[bank], i * ring.per + (turn + 1))
        return psum[:, bank, :], free[bank]

    def emptied(eng, ring, i, name):
        bank, turn = ring[name]
        eng.wait_ge(free[bank], i * ring.per + (turn + 2))

    block_context = nc.Block()
    block = block_context.__enter__()

    @block.sync
    def _(sp):
        def rows_of(a, i):
            return a[bass.ds(i * T, T), :].rearrange("(t p) d -> p t d", p=P)

        sp.dma_start(tab[:, :], tabs).then_inc(loaded, 16)
        sp.dma_start(xt[:, :, :], rows_of(x, 0)).then_inc(x_in, 16)
        for dst, src in ((col[:, :], cols), (wqkv_sb[:, :, :], wqkv), (wx_sb[:, :, :, :], wx),
                         (wo_sb[:, :, :], wo), (wr_sb[:, :, :], wr)):
            sp.dma_start(dst, src).then_inc(loaded, 16)
        sp.dma_start(ct[:, :, :], rows_of(ctx, 0)).then_inc(ctx_in, 16)
        sp.sem_inc(out_done, 16)
        sp.sem_inc(row_done, 16)

        def batch(i, last):
            if not last:
                emptied(sp, SUM_BANKS, i, "wo1")
                sp.dma_start(xt[:, :, :], rows_of(x, i + 1)).then_inc(x_in, 16)
                bank, turn = SUM_BANKS["vx1"]
                sp.wait_ge(full[bank], i * SUM_BANKS.per + (turn + 1))
                sp.dma_start(ct[:, :, :], rows_of(ctx, i + 1)).then_inc(ctx_in, 16)
            emptied(sp, SUM_BANKS, i, "h1")
            sp.dma_start(rows_of(out, i), x1[:, :, :]).then_inc(out_done, 16)
            sp.wait_ge(row_in, i + 1)
            sp.dma_start(rows_of(table, i), row[:, :, :]).then_inc(row_done, 16)

        with nc.sync.Fori(0, B - 1) as i:
            batch(i, False)
        batch(B - 1, True)
        sp.wait_ge(out_done, 16 * B + 16)
        sp.wait_ge(row_done, 16 * B + 16)

    @block.gpsimd
    def _(pool):
        nc.gpsimd.memset(half[:, :], -0.5).then_inc(zeroed, 1)
        nc.gpsimd.memset(kz[:, :, :, :], 0.0).then_inc(zeroed, 1)
        pool.wait_ge(zeroed, 2)
        with nc.gpsimd.Fori(0, B) as i:
            def root(n):
                t = n % TT
                pool.wait_ge(stats, i * (3 * TT) + (n + 1))
                alone(pool)
                nc.gpsimd.tensor_scalar(ve[:, t:t + 1], mv[:, t, 1:2], EPS, None, ALU.add).then_inc(ve_in, 1)
                pool.wait_ge(ve_in, i * (3 * TT) + (n + 1))
                nc.gpsimd.tensor_tensor(rstd[:, t:t + 1], ve[:, t:t + 1], half[:, 0:1], ALU.pow).then_inc(rooted, 1)

            for n in range(TT):
                root(n)
            for k in range(3 * TT):
                lo, n = ROPE_PARTS[k % 3]
                if k % 3 < 2:
                    emptied(pool, SUM_BANKS, i, ("qa", "qb")[k % 3] + str(k // 3))
                else:
                    pool.wait_ge(k_roped, i * TT + (k // 3 + 1))
                nc.gpsimd.tensor_tensor(qk[:, k // 3, lo:lo + n], rope1[:, k % 2, 0:n], rope2[:, k % 2, 0:n],
                                        ALU.add).then_inc(rope_sum, 1)
            emptied(pool, SUM_BANKS, i, "gvar")
            nc.gpsimd.tensor_tensor(grs[:, :], gve[:, :], half[:, :], ALU.pow).then_inc(groot, 1)
            for n in range(TT, 2 * TT):
                root(n)
            for q in range(4):
                pool.wait_ge(xrec, i * 4 + (q + 1))
                alone(pool)
                nc.gpsimd.tensor_scalar(pr[:, q, :], pr[:, q, :], rdenx[:, q:q + 1], None, ALU.mult).then_inc(xnorm, 1)
            for n in range(2 * TT, 3 * TT):
                root(n)

    @block.scalar
    def _(act):
        act.wait_ge(made, 3)
        nc.scalar.activation(lam[:, :], dots[:, :], ACT.Exp).then_inc(lam_exp, 1)
        with nc.scalar.Fori(0, B) as i:
            for t in range(TT):
                ps, freed = filled(act, SUM_BANKS, i, f"kv{t}")
                act.wait_ge(k_roped, i * TT + (t + 1))
                nc.scalar.copy(v[:, t, :], ps[:, 256:512]).then_inc(freed, 1)
            for n in range(2):
                ps, freed = filled(act, SUM_BANKS, i, f"kx{n}")
                nc.scalar.activation(kx[:, n, :], ps, ACT.Identity, bias=col[:, KB + n:KB + n + 1]).then_inc(freed, 1)
            for n in range(4):
                ps, freed = filled(act, TURN_BANKS, i, f"qT{n}")
                nc.scalar.copy(qT[:, 2 * n:2 * n + 2, :], ps.rearrange("p (a b) -> p a b", a=2)).then_inc(freed, 1)

            def exponentials(j):
                act.wait_ge(max_in, i * UNITS + (j + 1))
                for t in range(TT):
                    for r in range(4):
                        bank, _ = SCORE_BANKS[f"s{j}" + ("A" if t == 0 else "BC"[r // 2])]
                        lo, n = (r * P, P) if t == 0 else (r % 2 * T, T)
                        k = 4 * t + r
                        ins = nc.scalar.activation(ex[:, j % 2, r, t * P:t * P + n], psum[:, bank, lo:lo + n], ACT.Exp,
                                                   bias=nm[:, j % 2, k:k + 1], scale=SCALE,
                                                   accum_out=den[:, j % 2, k:k + 1])
                        if r == 3 or (t == 1 and r == 1):
                            ins.then_inc(free[bank], 1)

            def turned(j):
                for h in range(2):
                    ps, freed = filled(act, TURN_BANKS, i, f"dT{j}{h}")
                    nc.scalar.copy(diffT[:, j % 2, h, :], ps[:, 0:3 * P]).then_inc(freed, 1)

            for j in range(UNITS + 1):
                if j < UNITS:
                    exponentials(j)
                if j >= 1:
                    turned(j - 1)
            for n in range(2):
                ps, freed = filled(act, SUM_BANKS, i, f"vx{n}")
                nc.scalar.copy(vx[:, 2 * n:2 * n + 2, :], ps.rearrange("p (a b) -> p a b", a=2)).then_inc(freed, 1)
            for n in range(2):
                ps, freed = filled(act, SUM_BANKS, i, f"qx{n}")
                nc.scalar.activation(qx[:, n, :], ps, ACT.Identity, bias=col[:, QB + n:QB + n + 1]).then_inc(freed, 1)
            for q in range(4):
                act.wait_ge(xmax, i * 4 + (q + 1))
                bank, _ = SCORE_BANKS[f"x{q}"]
                nc.scalar.activation(pr[:, q, :], psum[:, bank, :], ACT.Exp, bias=nmx[:, q:q + 1], scale=1.0,
                                     accum_out=denx[:, q:q + 1]).then_inc(free[bank], 1)
            for q in (0, 2):
                ps, freed = filled(act, TURN_BANKS, i, f"pT{q}")
                nc.scalar.copy(prT[:, :, q * P:(q + 1) * P], ps.rearrange("p (a b) -> p a b", a=4)).then_inc(freed, 1)
            for t in range(TT):
                act.wait_ge(rmax_in, i * TT + (t + 1))
                bank, _ = SUM_BANKS[f"route{t}"]
                nc.scalar.activation(pexp[:, t, :], psum[:, bank, 0:EXPERTS], ACT.Exp, bias=rnm[:, t:t + 1], scale=1.0,
                                     accum_out=rden1[:, t:t + 1]).then_inc(free[bank], 1)

    @block.vector
    def _(dve):
        vec = nc.vector
        dve.wait_ge(loaded, 16 * 6)
        vec.tensor_tensor(prod[:, 0, :], col[:, LAM:LAM + DH], col[:, LAM + DH:LAM + 2 * DH], ALU.mult)
        vec.tensor_tensor(prod[:, 1, :], col[:, LAM + 2 * DH:LAM + 3 * DH], col[:, LAM + 3 * DH:LAM + 4 * DH],
                          ALU.mult).then_inc(made, 1)
        vec.tensor_scalar(gnw[:, :], col[:, GW:GW + UNITS], 1.0 - LAMBDA_INIT, None, ALU.mult)
        vec.tensor_scalar(gnb[:, :], col[:, GB:GB + UNITS], 1.0 - LAMBDA_INIT, None, ALU.mult)
        vec.tensor_copy(ident_b[:, :], ident)
        vec.tensor_copy(tri_b[:, :, :], tab[:, TRI:TRI + 4 * P].rearrange("p (a b) -> p a b", a=4)).then_inc(made, 1)
        dve.wait_ge(made, 2)
        vec.tensor_reduce(dots[:, :], prod[:, :, :], AX.X, ALU.add).then_inc(made, 1)
        vec.tensor_copy(keycol[:, :], tab[:, KEY0:KEY0 + TT]).then_inc(made, 1)
        dve.wait_ge(lam_exp, 1)
        vec.scalar_tensor_tensor(out=neglam[:, :], in0=lam[:, 1:2], scalar=LAMBDA_INIT, in1=lam[:, 0:1],
                                 op0=ALU.subtract, op1=ALU.subtract).then_inc(made, 1)
        dve.wait_ge(made, 5)
        dve.wait_ge(zeroed, 2)
        with nc.vector.Fori(0, B) as i:
            steps = [0]

            def mark(ins):
                steps[0] += 1
                ins.then_inc(step, 1)
                return steps[0]

            def seen(n):
                dve.wait_ge(step, i * DVE_STEPS + n)

            def layernorm(n, src, dst):
                t = n % TT
                seen(mark(vec.bn_stats(st6[:, t, :], src)))
                alone(dve)
                vec.bn_aggr(mv[:, t, :], st6[:, t, :]).then_inc(stats, 1)
                dve.wait_ge(rooted, i * (3 * TT) + (n + 1))
                vec.tensor_scalar(dst, src, mv[:, t, 0:1], rstd[:, t:t + 1], ALU.subtract, ALU.mult).then_inc(normed, 1)

            dve.wait_ge(x_in, i * 16 + 16)
            for t in range(TT):
                layernorm(t, xt[:, t, :], xn[:, t, :])
            for n in range(2):
                ps, freed = filled(dve, TURN_BANKS, i, f"xnT{n}")
                vec.tensor_copy(xnT[:, 2 * n:2 * n + 2, :], ps.rearrange("p (a b) -> p a b", a=2)).then_inc(freed, 1)
            for k in range(3 * TT):
                t, part = divmod(k, 3)
                ps, freed = filled(dve, SUM_BANKS, i, ("qa", "qb", "kv")[part] + str(t))
                if k >= 2:
                    dve.wait_ge(rope_sum, i * (3 * TT) + (k - 1))
                n = ROPE_PARTS[part][1]
                g = n // DH
                src = ps[:, 0:n].rearrange("p (g d) -> p g d", d=DH)
                a = rope1[:, k % 2, 0:n].rearrange("p (g d) -> p g d", d=DH)
                b = rope2[:, k % 2, 0:n].rearrange("p (g d) -> p g d", d=DH)
                cos = tab[:, COS + t * DH:COS + (t + 1) * DH]
                sin = tab[:, SIN + t * DH:SIN + (t + 1) * DH]
                h = DH // 2
                vec.tensor_tensor(b[:, :, 0:h], src[:, :, h:DH], sin[:, 0:h].unsqueeze(1).broadcast_to([P, g, h]), ALU.mult)
                vec.tensor_tensor(b[:, :, h:DH], src[:, :, 0:h], sin[:, h:DH].unsqueeze(1).broadcast_to([P, g, h]), ALU.mult)
                ins = vec.tensor_tensor(a, src, cos.unsqueeze(1).broadcast_to([P, g, DH]), ALU.mult)
                ins.then_inc(freed if part < 2 else k_roped, 1)
            ps, freed = filled(dve, TURN_BANKS, i, "kT")
            for r in range(4):
                q = slice(32 * r, 32 * r + 32)
                ins = vec.tensor_copy(kz[q, :, r, :], ps[q, :].rearrange("p (a b) -> p a b", a=2))
            ins.then_inc(freed, 1)

            def maxima(j):
                for part, at in zip("ABC", (0, 4, 6)):
                    ps, _ = filled(dve, SCORE_BANKS, i, f"s{j}{part}")
                    n = 4 if part == "A" else 2
                    ins = vec.tensor_reduce(mx[:, j % 2, at:at + n], ps.rearrange("p (a b) -> p a b", a=n), AX.X, ALU.max)
                seen(mark(ins))
                vec.tensor_scalar(nm[:, j % 2, :], mx[:, j % 2, :], -SCALE, None, ALU.mult).then_inc(max_in, 1)

            def difference(j):
                if j >= 2:
                    emptied(dve, SUM_BANKS, i, f"pv{j - 2}")
                emptied(dve, SCORE_BANKS, i, f"s{j}C")
                seen(mark(vec.reciprocal(rden[:, j % 2, :], den[:, j % 2, :])))
                d = den[:, j % 2, :].rearrange("p (a i) -> p a i", i=2)
                rd = rden[:, j % 2, :].rearrange("p (a i) -> p a i", i=2)
                seen(mark(vec.scalar_tensor_tensor(out=cmul[:, j % 2, :], in0=rd[:, :, 1], scalar=neglam[:, 0:1],
                                                   in1=d[:, :, 0], op0=ALU.mult, op1=ALU.mult)))
                for t in range(TT):
                    for h in range(2):
                        s = slice(t * P, P + 2 * t * P)
                        ins = vec.scalar_tensor_tensor(out=diff[:, j % 2, h, s], in0=ex[:, j % 2, 2 * h + 1, s],
                                                       scalar=cmul[:, j % 2, 2 * t + h:2 * t + h + 1],
                                                       in1=ex[:, j % 2, 2 * h, s], op0=ALU.mult, op1=ALU.add)
                ins.then_inc(diff_in, 1)

            def scaled(j):
                ps, freed = filled(dve, SUM_BANKS, i, f"pv{j}")
                r1 = rden[:, j % 2, :].rearrange("p (a i) -> p a i", i=2)[:, :, 0:1].broadcast_to([P, 4, HD])
                vec.tensor_tensor(osc[:, j % 2, :, :].rearrange("p t (h d) -> p (t h) d", h=2),
                                  ps[:, 0:T].rearrange("p (a d) -> p a d", d=HD), r1, ALU.mult).then_inc(freed, 1)

            def collected(j):
                ps, freed = filled(dve, SUM_BANKS, i, f"oT{j}")
                vec.bn_stats(go6[:, j, :], ps[:, 0:T])
                vec.tensor_copy(oT[:, j, :], ps[:, 0:T]).then_inc(freed, 1)

            for s in range(UNITS + 4):
                if s < UNITS:
                    maxima(s)
                if 1 <= s <= UNITS:
                    difference(s - 1)
                if s >= 4:
                    collected(s - 4)
                if 2 <= s < UNITS + 2:
                    scaled(s - 2)
            emptied(dve, SUM_BANKS, i, f"oT{UNITS - 1}")
            alone(dve)
            for j in range(UNITS):
                ins = vec.bn_aggr(gmv[:, j, :], go6[:, j, :])
            ins.then_inc(gstat, 1)
            ps, freed = filled(dve, SUM_BANKS, i, "gmean")
            seen(mark(vec.tensor_copy(gm[:, :], ps[:, 0:UNITS])))
            seen(mark(vec.tensor_tensor(gdev[:, :], gmv[:, :, 0], gm[:, :], ALU.subtract)))
            seen(mark(vec.tensor_tensor(gsq[:, :], gdev[:, :], gdev[:, :], ALU.mult)))
            vec.tensor_tensor(gdev[:, :], gsq[:, :], gmv[:, :, 1], ALU.add).then_inc(freed, 1)
            ps, freed = filled(dve, SUM_BANKS, i, "gvar")
            vec.tensor_scalar(gve[:, :], ps[:, 0:UNITS], EPS, None, ALU.add).then_inc(freed, 1)
            dve.wait_ge(groot, i + 1)
            seen(mark(vec.tensor_tensor(ga[:, :], grs[:, :], gnw[:, :], ALU.mult)))
            seen(mark(vec.tensor_tensor(gsq[:, :], gm[:, :], ga[:, :], ALU.mult)))
            seen(mark(vec.tensor_tensor(gb[:, :], gnb[:, :], gsq[:, :], ALU.subtract)))
            for j in range(UNITS):
                ins = vec.tensor_scalar(oT[:, j, :], oT[:, j, :], ga[:, j:j + 1], gb[:, j:j + 1], ALU.mult, ALU.add)
                if j == UNITS - 1:
                    ins.then_inc(gdone, 1)
            dve.wait_ge(out_done, i * 16 + 16)
            for t in range(TT):
                ps, freed = filled(dve, SUM_BANKS, i, f"wo{t}")
                vec.tensor_tensor(x1[:, t, :], xt[:, t, :], ps, ALU.add).then_inc(freed, 1)
                emptied(dve, SUM_BANKS, i, f"wo{t}")
                layernorm(TT + t, x1[:, t, :], xn[:, t, :])

            def xmaximum(q):
                ps, _ = filled(dve, SCORE_BANKS, i, f"x{q}")
                seen(mark(vec.tensor_reduce(mxx[:, q:q + 1], ps, AX.X, ALU.max)))
                vec.tensor_scalar(nmx[:, q:q + 1], mxx[:, q:q + 1], -1.0, None, ALU.mult).then_inc(xmax, 1)

            for q in range(4 + 1):
                if q < 4:
                    xmaximum(q)
                if q >= 1:
                    emptied(dve, SCORE_BANKS, i, f"x{q - 1}")
                    vec.reciprocal(rdenx[:, q - 1:q], denx[:, q - 1:q]).then_inc(xrec, 1)
            for q in (1, 3):
                ps, freed = filled(dve, TURN_BANKS, i, f"pT{q}")
                vec.tensor_copy(prT[:, :, q * P:(q + 1) * P], ps.rearrange("p (a b) -> p a b", a=4)).then_inc(freed, 1)
            dve.wait_ge(row_done, i * 16 + 16)
            for t in range(TT):
                ps, freed = filled(dve, SUM_BANKS, i, f"h{t}")
                vec.scalar_tensor_tensor(out=x1[:, t, :], in0=ps, scalar=col[:, VB + t:VB + t + 1], in1=x1[:, t, :],
                                         op0=ALU.add, op1=ALU.add).then_inc(freed, 1)
                emptied(dve, SUM_BANKS, i, f"h{t}")
                layernorm(2 * TT + t, x1[:, t, :], row[:, t, 0:D])
            for n in range(2):
                ps, freed = filled(dve, TURN_BANKS, i, f"rT{n}")
                vec.tensor_copy(rT[:, 2 * n:2 * n + 2, :], ps.rearrange("p (a b) -> p a b", a=2)).then_inc(freed, 1)
            for t in range(TT):
                ps, _ = filled(dve, SUM_BANKS, i, f"route{t}")
                seen(mark(vec.tensor_reduce(rmx[:, t:t + 1], ps[:, 0:EXPERTS], AX.X, ALU.max)))
                vec.tensor_scalar(rnm[:, t:t + 1], rmx[:, t:t + 1], -1.0, None, ALU.mult).then_inc(rmax_in, 1)
            emptied(dve, SUM_BANKS, i, "route0")
            emptied(dve, SUM_BANKS, i, "route1")
            seen(mark(vec.reciprocal(rr[:, :], rden1[:, :])))
            vec.tensor_scalar(prob[:, 0, :], pexp[:, 0, :], rr[:, 0:1], None, ALU.mult)
            seen(mark(vec.tensor_scalar(prob[:, 1, :], pexp[:, 1, :], rr[:, 1:2], None, ALU.mult)))
            alone(dve)
            vec.max(top[:, 0, :], prob[:, 0, :])
            seen(mark(vec.max(top[:, 1, :], prob[:, 1, :])))
            seen(mark(vec.tensor_reduce(s8[:, :], top[:, :, :], AX.X, ALU.add)))
            vec.reciprocal(r8[:, :], s8[:, :])
            vec.match_replace(rest[:, 0, :], top[:, 0, :], prob[:, 0, :], -1.0)
            seen(mark(vec.match_replace(rest[:, 1, :], top[:, 1, :], prob[:, 1, :], -1.0)))
            seen(mark(vec.tensor_scalar(chosen[:, :, :], rest[:, :, :], 0.0, None, ALU.is_lt)))
            for t in range(TT):
                vec.tensor_scalar(keyed[:, t, :], chosen[:, t, :], keycol[:, t:t + 1], None, ALU.mult)
                ins = vec.scalar_tensor_tensor(out=row[:, t, D:ROW], in0=prob[:, t, :], scalar=r8[:, t:t + 1],
                                               in1=chosen[:, t, :], op0=ALU.mult, op1=ALU.mult)
            ins.then_inc(row_in, 1)
            ps, freed = filled(dve, TURN_BANKS, i, "keyT")
            mark(vec.tensor_scalar(keycol[:, :], keycol[:, :], -1.0, None, ALU.add))
            vec.tensor_copy(keys[:, bass.ds(i * P, P)], ps[:, 0:P]).then_inc(freed, 1)
            assert steps[0] == DVE_STEPS, steps

    @block.tensor
    def _(pe):
        for n in range(8):
            pe.sem_inc(free[n], 1)
        pe.wait_ge(loaded, 16 * 6)
        pe.wait_ge(made, 2)
        with nc.tensor.Fori(0, B) as i:
            def mm(out_, lhsT, rhs, start, stop):
                return nc.tensor.matmul(out_, lhsT, rhs, start=start, stop=stop)

            def turn(name, pieces):
                ps, done = begin(pe, TURN_BANKS, i, name)
                for n, piece in enumerate(pieces):
                    ins = nc.tensor.transpose(ps[:, n * P:(n + 1) * P], piece, ident)
                ins.then_inc(done, 1)

            def product(name, pairs, lo=0, n=BANK, end=True):
                ps, done = begin(pe, SUM_BANKS, i, name) if lo == 0 else (psum[:, SUM_BANKS[name][0], :], full[SUM_BANKS[name][0]])
                for k, (lhsT, rhs) in enumerate(pairs):
                    ins = mm(ps[:, lo:lo + n], lhsT, rhs, k == 0, k == len(pairs) - 1)
                if end:
                    ins.then_inc(done, 1)

            pe.wait_ge(normed, i * (3 * TT) + TT)
            for n in range(2):
                turn(f"xnT{n}", [xn[:, t, c * P:(c + 1) * P] for c in (2 * n, 2 * n + 1) for t in range(TT)])
            emptied(pe, TURN_BANKS, i, "xnT0")
            emptied(pe, TURN_BANKS, i, "xnT1")
            for t in range(TT):
                for part, name in enumerate(("qa", "qb", "kv")):
                    product(f"{name}{t}", [(xnT[:, c, t * P:(t + 1) * P], wqkv_sb[:, c, part * BANK:(part + 1) * BANK])
                                           for c in range(KC)])
            pe.wait_ge(ctx_in, i * 16 + 16)
            for n in range(2):
                product(f"kx{n}", [(wx_sb[:, 1, t, n * P:(n + 1) * P], ct[:, t, :]) for t in range(TT)])
            pe.wait_ge(rope_sum, i * (3 * TT) + 3 * TT)
            turn("kT", [qk[:, t, (UNITS + g) * P:(UNITS + g + 1) * P] for g in range(2) for t in range(TT)])
            for n in range(4):
                turn(f"qT{n}", [qk[:, t, j * P:(j + 1) * P] for j in (2 * n, 2 * n + 1) for t in range(TT)])
            emptied(pe, TURN_BANKS, i, "kT")

            def scores(j):
                g = j // 4
                if j % 2 == 0:
                    emptied(pe, TURN_BANKS, i, f"qT{j // 2}")
                ps, done = begin(pe, SCORE_BANKS, i, f"s{j}A")
                mm(ps, qT[:, j, 0:P], kz[:, g, :, 0:P], True, False)
                mm(ps, ident_b[:, :], tri_b[:, :, :], False, True).then_inc(done, 1)
                for k, part in enumerate("BC"):
                    ps, done = begin(pe, SCORE_BANKS, i, f"s{j}{part}")
                    mm(ps, qT[:, j, P:2 * P], kz[:, g, 2 * k:2 * k + 2, :], True, False)
                    mm(ps.rearrange("p (a b) -> p a b", a=2)[:, :, P:2 * P], ident_b[:, :], tri_b[:, 0:2, :],
                       False, True).then_inc(done, 1)

            def turn_difference(j):
                pe.wait_ge(diff_in, i * UNITS + (j + 1))
                for h in range(2):
                    turn(f"dT{j}{h}", [diff[:, j % 2, h, n * P:(n + 1) * P] for n in range(3)])

            def weigh(j):
                emptied(pe, TURN_BANKS, i, f"dT{j}0")
                emptied(pe, TURN_BANKS, i, f"dT{j}1")
                ps, done = begin(pe, SUM_BANKS, i, f"pv{j}")
                for h in range(2):
                    vh = v[:, :, (2 * (j // 4) + h) * HD:(2 * (j // 4) + h + 1) * HD]
                    dT = diffT[:, j % 2, h, :]
                    mm(ps[:, h * HD:(h + 1) * HD], dT[:, 0:P], vh[:, 0, :], True, True)
                    mm(ps[:, P + h * HD:P + (h + 1) * HD], dT[:, P:2 * P], vh[:, 0, :], True, False)
                    ins = mm(ps[:, P + h * HD:P + (h + 1) * HD], dT[:, 2 * P:3 * P], vh[:, 1, :], False, True)
                ins.then_inc(done, 1)

            def turn_output(j):
                emptied(pe, SUM_BANKS, i, f"pv{j}")
                ps, done = begin(pe, SUM_BANKS, i, f"oT{j}")
                for t in range(TT):
                    ins = nc.tensor.transpose(ps[:, t * P:(t + 1) * P], osc[:, j % 2, t, :], ident)
                ins.then_inc(done, 1)

            for s in range(UNITS + 3):
                if s < UNITS:
                    scores(s)
                if 1 <= s <= UNITS:
                    turn_difference(s - 1)
                if 2 <= s < UNITS + 2:
                    weigh(s - 2)
                if s >= 3:
                    turn_output(s - 3)
            for n in range(2):
                for half_ in range(2):
                    lt = 2 * n + half_
                    product(f"vx{n}", [(ct[:, t, lt * P:(lt + 1) * P], wx_sb[:, 2, t, :]) for t in range(TT)],
                            half_ * T, T, half_ == 1)
            heads = tab[:, HEADS:HEADS + P]
            pe.wait_ge(gstat, i + 1)
            product("gmean", [(heads, gmv[:, :, 0])], 0, UNITS)
            emptied(pe, SUM_BANKS, i, "gmean")
            product("gvar", [(heads, gdev[:, :])], 0, UNITS)
            pe.wait_ge(gdone, i + 1)
            for t in range(TT):
                product(f"wo{t}", [(oT[:, j, t * P:(t + 1) * P], wo_sb[:, j, :]) for j in range(UNITS)])
            pe.wait_ge(normed, i * (3 * TT) + 2 * TT)
            for n in range(2):
                product(f"qx{n}", [(wx_sb[:, 0, t, n * P:(n + 1) * P], xn[:, t, :]) for t in range(TT)])
            for name in ("kx0", "kx1", "qx0", "qx1"):
                emptied(pe, SUM_BANKS, i, name)
            for q in range(4):
                ps, done = begin(pe, SCORE_BANKS, i, f"x{q}")
                mm(ps, qx[:, 0, q * P:(q + 1) * P], kx[:, 0, :], True, False)
                mm(ps, qx[:, 1, q * P:(q + 1) * P], kx[:, 1, :], False, True).then_inc(done, 1)
            for q in range(4):
                pe.wait_ge(xnorm, i * 4 + (q + 1))
                turn(f"pT{q}", [pr[:, q, k * P:(k + 1) * P] for k in range(4)])
            for name in ("pT2", "pT3"):
                emptied(pe, TURN_BANKS, i, name)
            for n in range(2):
                product(f"h{n}", [(vx[:, k, n * P:(n + 1) * P], prT[:, k, :]) for k in range(4)])
            pe.wait_ge(normed, i * (3 * TT) + 3 * TT)
            for n in range(2):
                turn(f"rT{n}", [row[:, t, c * P:(c + 1) * P] for c in (2 * n, 2 * n + 1) for t in range(TT)])
            emptied(pe, TURN_BANKS, i, "rT0")
            emptied(pe, TURN_BANKS, i, "rT1")
            for t in range(TT):
                product(f"route{t}", [(rT[:, c, t * P:(t + 1) * P], wr_sb[:, c, :]) for c in range(KC)], 0, EXPERTS)
            pe.wait_ge(row_in, i + 1)
            turn("keyT", [keyed[:, :, :].rearrange("p a b -> p (a b)")])

    block_context.__exit__(None, None, None)


def experts(nc, st, psum, w13, w2, out, table, keys, tab):
    def sb(name, shape, dt=FP32):
        return st.enter_context(nc.sbuf_tensor(name, shape, dt))

    def sem(name):
        return st.enter_context(nc.semaphore(name))

    SLOTS = 4
    w13_sb = [sb(f"w13_sb{n}", [P, KC, 2 * FF]) for n in range(SLOTS)]
    w2a_sb = [sb(f"w2a_sb{n}", [P, D]) for n in range(SLOTS)]
    w2b_sb = [sb(f"w2b_sb{n}", [FF - P, D]) for n in range(SLOTS)]
    ident = tab[:, IDENT:IDENT + P]
    firsts = sb("firsts", [P, CAP])
    both = sb("both", [EXPERTS, 2 * CAP])
    slot = sb("slot", [EXPERTS, CAP])
    sloti, low, high = (sb(n, [EXPERTS, CAP], I32) for n in ("sloti", "low", "high"))
    held = sb("held", [EXPERTS, CAP])
    rowf = sb("rowf", [EXPERTS, 2, CAP])
    tmp, rows_to = sb("tmp", [EXPERTS, CAP]), sb("rows_to", [EXPERTS, CAP])
    from_idx = sb("from_idx", [P, PAIRS], I32)
    to_idx = sb("to_idx", [CAP, EXPERTS], I32)
    gidx = [sb(f"gidx{n}", [P, 1], I32) for n in range(2)]
    sidx = [sb(f"sidx{n}", [CAP, 1], I32) for n in range(2)]
    gx = [sb(f"gx{n}", [P, ROW]) for n in range(2)]
    wcol = [sb(f"wcol{n}", [P, 1]) for n in range(2)]
    gxT = [sb(f"gxT{n}", [P, KC, P]) for n in range(2)]
    eh, sig, gate = sb("eh", [P, FF]), sb("sig", [P, FF]), sb("gate", [P, FF])
    g = [sb(f"g{n}", [P, FF]) for n in range(2)]
    gT = [sb(f"gT{n}", [P, 2, P]) for n in range(2)]
    y = [sb(f"y{n}", [P, D]) for n in range(2)]
    zeros = sb("zeros", [CAP, D])

    pick, joined = sem("pick"), sem("joined")
    picked_out, rows_in, index_in = sem("picked_out"), sem("rows_in"), sem("index_in")
    zero_in, zero_out = sem("zero_in"), sem("zero_out")
    w_in = [sem(f"w_in{n}") for n in range(SLOTS)]
    idx_in, sidx_in, added = sem("idx_in"), sem("sidx_in"), sem("added")
    gx_in = [sem(f"gx_in{n}") for n in range(2)]
    gx_turned, gxT_in, wcol_in = sem("gx_turned"), sem("gxT_in"), sem("wcol_in")
    hidden, eh_in, g_in, g_turned, gT_in, y_full, y_in = (
        sem(n) for n in ("hidden", "eh_in", "g_in", "g_turned", "gT_in", "y_full", "y_in"))
    moe_step = sem("moe_step")

    turn_ps = [psum[:, n, :] for n in range(2)]
    hidden_ps = [psum[:, 2 + n, 0:2 * FF] for n in range(2)]
    gate_ps = [psum[:, 4 + n, 0:2 * P] for n in range(2)]
    y_ps = [psum[:, 6 + n, :] for n in range(2)]

    with nc.Block() as block:
        @block.sync
        def _(sp):
            def weights(e, n):
                sp.dma_start(w13_sb[n][:, :, :], w13[bass.ds(e * P, P), :].rearrange("p (c f) -> p c f", c=KC)).then_inc(w_in[n], 16)
                sp.dma_start(w2a_sb[n][:, :], w2[bass.ds(e * FF, P), :]).then_inc(w_in[n], 16)
                sp.dma_start(w2b_sb[n][:, :], w2[bass.ds(e * FF + P, FF - P), :]).then_inc(w_in[n], 16)

            for n in range(SLOTS):
                weights(n, n)
            sp.wait_ge(zero_in, 1)
            sp.dma_start(out[TOKENS:TOKENS + CAP, :], zeros[:, :]).then_inc(zero_out, 16)
            sp.wait_ge(pick, 8)
            sp.dma_start(both[:, 0:CAP], firsts[0:EXPERTS, :]).then_inc(joined, 16)
            sp.dma_start(both[:, CAP:2 * CAP], firsts[EXPERTS:P, :]).then_inc(joined, 16)
            with nc.sync.Fori(0, EXPERTS // SLOTS - 1) as i:
                for n in range(SLOTS):
                    sp.wait_ge(y_full, i * 2 + (n // 2 + 1))
                    weights(i * SLOTS + (SLOTS + n), n)

        @block.gpsimd
        def _(pool):
            nc.gpsimd.memset(zeros[:, :], 0.0).then_inc(zero_in, 1)
            pool.wait_ge(zero_out, 16)
            pool.wait_ge(index_in, 2)

            def fetch(k, n):
                nc.gpsimd.tensor_copy(gidx[n][:, :], from_idx[:, bass.ds(k, 1)]).then_inc(idx_in, 1)
                pool.wait_ge(idx_in, k + 1)
                alone(pool)
                nc.gpsimd.indirect_dma_start(
                    out=gx[n][:, :], out_offset=None, in_=table,
                    in_offset=bass.IndirectOffsetOnAxis(ap=gidx[n][:, 0:1], axis=0)).then_inc(gx_in[n], 16)

            def add(i, n):
                k = 2 * i + n
                pool.wait_ge(y_in, k + 1)
                alone(pool)
                for h in range(2):
                    nc.gpsimd.tensor_copy(sidx[h][:, :], to_idx[:, bass.ds(2 * k + h, 1)]).then_inc(sidx_in, 1)
                for h in range(2):
                    pool.wait_ge(sidx_in, 2 * k + 2)
                    if h:
                        pool.wait_ge(added, 32 * k + 16)
                    alone(pool)
                    nc.gpsimd.indirect_dma_start(
                        out=out, out_offset=bass.IndirectOffsetOnAxis(ap=sidx[h][:, 0:1], axis=0),
                        in_=y[n][h * CAP:(h + 1) * CAP, :], in_offset=None, compute_op=ALU.add).then_inc(added, 16)
                pool.wait_ge(added, 32 * k + 32)
                alone(pool)

            fetch(0, 0)
            fetch(1, 1)
            with nc.gpsimd.Fori(0, PAIRS // 2 - 1) as i:
                for n in range(2):
                    add(i, n)
                    fetch(2 * i + n + 2, n)
            for n in range(2):
                add(PAIRS // 2 - 1, n)

        @block.scalar
        def _(act):
            with nc.scalar.Fori(0, PAIRS // 2) as i:
                for n in range(2):
                    k = 2 * i + n
                    act.wait_ge(gx_turned, k + 1)
                    nc.scalar.copy(gxT[n][:, :, :], turn_ps[n].rearrange("p (c s) -> p c s", c=KC)).then_inc(gxT_in, 1)
                    act.wait_ge(hidden, k + 1)
                    nc.scalar.activation(eh[:, :], hidden_ps[n][:, 0:FF], ACT.Exp, scale=-1.0).then_inc(eh_in, 1)
                    act.wait_ge(g_turned, k + 1)
                    nc.scalar.copy(gT[n][:, 0, :], gate_ps[n][:, 0:P])
                    nc.scalar.copy(gT[n][0:FF - P, 1, :], gate_ps[n][0:FF - P, P:2 * P]).then_inc(gT_in, 1)

        @block.vector
        def _(dve):
            vec = nc.vector

            rounds = CAP // 8

            def earliest(src, dst, call):
                for r in range(rounds):
                    vec.max(dst[:, 8 * r:8 * r + 8], src).then_inc(pick, 1)
                    dve.wait_ge(pick, call * rounds + r + 1)
                    if r < rounds - 1:
                        vec.match_replace(src, dst[:, 8 * r:8 * r + 8], src, 0.0).then_inc(picked_out, 1)
                        dve.wait_ge(picked_out, call * (rounds - 1) + r + 1)

            earliest(keys[:, :], firsts[:, :], 0)
            dve.wait_ge(joined, 32)
            earliest(both[:, :], slot[:, :], 1)
            done = [0]

            def then(ins):
                done[0] += 1
                ins.then_inc(rows_in, 1)
                dve.wait_ge(rows_in, done[0])

            then(vec.tensor_scalar(sloti[:, :], slot[:, :], -1.0, float(TOKENS), ALU.mult, ALU.add))
            then(vec.tensor_scalar(low[:, :], sloti[:, :], B - 1, 8, ALU.bitwise_and, ALU.logical_shift_left))
            then(vec.tensor_scalar(high[:, :], sloti[:, :], 4, T - 1, ALU.logical_shift_right, ALU.bitwise_and))
            then(vec.tensor_tensor(tmp[:, :], low[:, :], high[:, :], ALU.add))
            then(vec.tensor_scalar(held[:, :], slot[:, :], 0.5, None, ALU.is_gt))
            then(vec.tensor_tensor(rowf[:, 0, :], tmp[:, :], held[:, :], ALU.mult))
            then(vec.tensor_copy(rowf[:, 1, :], rowf[:, 0, :]))
            then(vec.tensor_tensor(tmp[:, :], tab[0:EXPERTS, SPARE:SPARE + CAP], held[:, :], ALU.mult))
            then(vec.tensor_tensor(tmp[:, :], tab[0:EXPERTS, SPARE:SPARE + CAP], tmp[:, :], ALU.subtract))
            then(vec.tensor_tensor(rows_to[:, :], tmp[:, :], rowf[:, 0, :], ALU.add))
            dve.wait_ge(index_in, 1)
            dup = turn_ps[0][:, 0:EXPERTS].rearrange("p (k e) -> p k e", e=2)
            vec.tensor_copy(from_idx[0:CAP, :], dup[0:CAP, :, 0])
            vec.tensor_copy(from_idx[CAP:P, :], dup[CAP:P, :, 1])
            vec.tensor_copy(to_idx[:, :], turn_ps[1][0:CAP, 0:EXPERTS]).then_inc(index_in, 1)
            with nc.vector.Fori(0, PAIRS // 2) as i:
                for m in range(2):
                    k = 2 * i + m
                    dve.wait_ge(gx_in[m], i * 16 + 16)
                    alone(dve)
                    vec.tensor_copy(wcol[m][0:CAP, :], gx[m][0:CAP, bass.ds(D + 2 * k, 1)])
                    vec.tensor_copy(wcol[m][CAP:P, :], gx[m][CAP:P, bass.ds(D + 1 + 2 * k, 1)]).then_inc(wcol_in, 1)
                    dve.wait_ge(eh_in, k + 1)
                    alone(dve)
                    vec.tensor_scalar(sig[:, :], eh[:, :], 1.0, None, ALU.add).then_inc(moe_step, 1)
                    dve.wait_ge(moe_step, 3 * k + 1)
                    vec.reciprocal(gate[:, :], sig[:, :]).then_inc(moe_step, 1)
                    dve.wait_ge(moe_step, 3 * k + 2)
                    vec.tensor_tensor(sig[:, :], hidden_ps[m][:, 0:FF], gate[:, :], ALU.mult).then_inc(moe_step, 1)
                    dve.wait_ge(moe_step, 3 * k + 3)
                    vec.tensor_tensor(g[m][:, :], hidden_ps[m][:, FF:2 * FF], sig[:, :], ALU.mult).then_inc(g_in, 1)
                    dve.wait_ge(wcol_in, k + 1)
                    dve.wait_ge(y_full, k + 1)
                    vec.tensor_scalar(y[m][:, :], y_ps[m], wcol[m][:, 0:1], None, ALU.mult).then_inc(y_in, 1)

        @block.tensor
        def _(pe):
            mm = nc.tensor.matmul
            pe.wait_ge(rows_in, 10)
            nc.tensor.transpose(turn_ps[0][:, 0:EXPERTS], rowf[:, :, :].rearrange("e a s -> e (a s)"), ident[0:EXPERTS, 0:EXPERTS])
            nc.tensor.transpose(turn_ps[1][0:CAP, 0:EXPERTS], rows_to[:, :], ident[0:EXPERTS, 0:EXPERTS]).then_inc(index_in, 1)
            pe.wait_ge(index_in, 2)
            with nc.tensor.Fori(0, PAIRS // 2) as i:
                for n in range(2):
                    k = 2 * i + n
                    pe.wait_ge(gx_in[n], i * 16 + 16)
                    for c in range(KC):
                        ins = nc.tensor.transpose(turn_ps[n][:, c * P:(c + 1) * P], gx[n][:, c * P:(c + 1) * P], ident)
                    ins.then_inc(gx_turned, 1)
                    pe.wait_ge(gxT_in, k + 1)
                    for h in range(2):
                        pe.wait_ge(w_in[2 * n + h], i * 48 + 48)
                    alone(pe)
                    for c in range(KC):
                        for h in range(2):
                            ins = mm(hidden_ps[n][h * CAP:(h + 1) * CAP, :], gxT[n][:, c, h * CAP:(h + 1) * CAP],
                                     w13_sb[2 * n + h][:, c, :], start=(c == 0), stop=(c == KC - 1), skip_group_check=True)
                    ins.then_inc(hidden, 1)
                    pe.wait_ge(g_in, k + 1)
                    nc.tensor.transpose(gate_ps[n][:, 0:P], g[n][:, 0:P], ident)
                    nc.tensor.transpose(gate_ps[n][0:FF - P, P:2 * P], g[n][:, P:FF], ident).then_inc(g_turned, 1)
                    pe.wait_ge(gT_in, k + 1)
                    alone(pe)
                    for h in range(2):
                        s = slice(h * CAP, (h + 1) * CAP)
                        mm(y_ps[n][s, :], gT[n][:, 0, s], w2a_sb[2 * n + h][:, :], start=True, stop=False, skip_group_check=True)
                    for h in range(2):
                        s = slice(h * CAP, (h + 1) * CAP)
                        ins = mm(y_ps[n][s, :], gT[n][0:FF - P, 1, s], w2b_sb[2 * n + h][:, :], start=False, stop=True,
                                 skip_group_check=True)
                    ins.then_inc(y_full, 1)


def constants():
    tabs = np.zeros((P, TAB), np.float32)
    tabs[:, IDENT:IDENT + P] = np.eye(P)
    tri = np.where(np.arange(P)[None, :] > np.arange(P)[:, None], MASKED, 0.0)
    tabs[:, TRI:TRI + 4 * P] = np.tile(tri, (1, 4))
    tabs[:, HEADS:HEADS + P] = np.kron(np.eye(P // HD), np.full((HD, HD), 1.0 / HD))
    inv = (1.0 / np.float32(10000.0) ** (np.arange(0, DH, 2, dtype=np.float32) / np.float32(DH))).astype(np.float32)
    angle = (np.arange(T, dtype=np.float32)[:, None] * inv[None, :]).astype(np.float32).astype(np.float64)
    for t in range(TT):
        a = angle[t * P:(t + 1) * P]
        tabs[:, COS + t * DH:COS + (t + 1) * DH] = np.concatenate([np.cos(a), np.cos(a)], 1)
        tabs[:, SIN + t * DH:SIN + (t + 1) * DH] = np.concatenate([-np.sin(a), np.sin(a)], 1)
        tabs[:, KEY0 + t] = TOKENS - B * (t * P + np.arange(P))
    tabs[:, SPARE:SPARE + CAP] = TOKENS + np.arange(CAP)
    return tabs


def chunks(w):
    return np.ascontiguousarray(w.reshape(-1, P, w.shape[-1]).transpose(1, 0, 2))


def kernel(x, ctx_2048, L0_attn_Wq, L0_attn_Wk, L0_attn_Wv, L0_attn_Wo, L0_attn_lambda_q1, L0_attn_lambda_k1,
           L0_attn_lambda_q2, L0_attn_lambda_k2, L0_attn_gn_w, L0_attn_gn_b, L0_xattn_QW, L0_xattn_Qb, L0_xattn_KW,
           L0_xattn_Kb, L0_xattn_VW, L0_xattn_Vb, L0_ffn_router_w, L0_ffn_w1, L0_ffn_v1, L0_ffn_w2):
    import concourse.bacc as bacc
    from concourse.bass_utils import run_bass_kernel_spmd

    heads = np.array([[4 * (2 * (j // 4) + h) + j % 4 for h in range(2)] for j in range(UNITS)]).reshape(-1)
    pairs = np.concatenate([np.arange(0, DH, 2), np.arange(1, DH, 2)])
    inner = np.concatenate([i * DH + pairs for i in range(2)])
    q_cols = (heads[:, None] * HD + inner[None, :]).reshape(-1)
    k_cols = (np.arange(KV)[:, None] * HD + inner[None, :]).reshape(-1)
    o_rows = (heads[:, None] * HD + np.arange(HD)[None, :]).reshape(-1)
    a = {k: np.asarray(w) for k, w in locals().items() if k.startswith("L0_")}

    def columns(v):
        return v.reshape(-1, P).T

    lams = np.concatenate([a[f"L0_attn_lambda_{n}"] for n in ("q1", "k1", "q2", "k2")])
    cols = np.concatenate([columns(a["L0_attn_gn_w"][o_rows]), columns(a["L0_attn_gn_b"][o_rows]),
                           columns(a["L0_xattn_Qb"]), columns(a["L0_xattn_Kb"]), columns(a["L0_xattn_Vb"]),
                           np.broadcast_to(lams, (P, 4 * DH))], axis=1)
    w13 = np.concatenate([a["L0_ffn_w1"], a["L0_ffn_v1"]], axis=1)
    w13 = w13.transpose(0, 2, 1).reshape(EXPERTS, KC, P, 2 * FF).transpose(0, 2, 1, 3)
    arrays = {
        "x": np.asarray(x).reshape(TOKENS, D),
        "ctx": np.asarray(ctx_2048).reshape(TOKENS, D),
        "wqkv": chunks(np.concatenate([a["L0_attn_Wq"][:, q_cols], a["L0_attn_Wk"][:, k_cols], a["L0_attn_Wv"]], 1)),
        "wo": chunks(a["L0_attn_Wo"][o_rows]),
        "wx": np.stack([chunks(a[f"L0_xattn_{n}W"].T) for n in "QKV"], 1),
        "wr": chunks(a["L0_ffn_router_w"].T),
        "cols": cols,
        "tabs": constants(),
        "w13": w13.reshape(EXPERTS * P, KC * 2 * FF),
        "w2": a["L0_ffn_w2"].reshape(EXPERTS * FF, D),
    }
    arrays = {k: np.ascontiguousarray(v) for k, v in arrays.items()}
    nc = bacc.Bacc("TRN2", target_bir_lowering=False, num_devices=1)
    args = [nc.dram_tensor(k, v.shape, FP32, kind="ExternalInput").ap() for k, v in arrays.items()]
    out = nc.dram_tensor("out", (TOKENS + CAP, D), FP32, kind="ExternalOutput").ap()
    table = nc.dram_tensor("table", (TOKENS, ROW), FP32, kind="Internal").ap()
    build(nc, *args, out, table)
    r = run_bass_kernel_spmd(nc, [arrays], core_ids=[0])
    return r.results[0]["out"][:TOKENS].reshape(B, T, D)
```

```python
import math
from contextlib import ExitStack

import numpy as np

import concourse.bass as bass
from concourse import mybir

FP32 = mybir.dt.float32
BF16 = mybir.dt.bfloat16
I32 = mybir.dt.int32
ALU = mybir.AluOpType
ACT = mybir.ActivationFunctionType
AX = mybir.AxisListType

P = 128
B, T, D = 16, 256, 512
H, KV, DH = 16, 4, 32
TT = T // P
KC = D // P
HD = 2 * DH
UNITS = H // 2
NQK = 2 * H * DH + 2 * KV * DH
NQKV = NQK + KV * HD
ROPE_PARTS = [(0, 512), (512, 512), (1024, 256)]
BANK = 512
EXPERTS, TOPK, FF, CAP = 64, 8, 192, 64
TOKENS = B * T
ROW = D + EXPERTS
PAIRS = EXPERTS // 2
LAMBDA_INIT = 0.8 - 0.6 * math.exp(0.0)
EPS = 1e-5
SCALE = 1.0 / math.sqrt(DH)
MASKED = -1e30
STEPS = [0, 2, 30, 8, 9]

IDENT, TRI, HEADS, COS, SIN, KEY0, SPARE, TAB = 0, 128, 640, 768, 832, 896, 898, 962
GW, GB, QB, KB, VB, LAM, COLS = 0, 8, 16, 18, 20, 22, 150


class Ring:

    def __init__(self, banks, names, before, lead, per, r):
        self.names, self.done, self.at = names, 0, {}
        before = dict(before)
        for n, name in enumerate(names):
            bank = banks[(lead + n) % len(banks)]
            before[bank] = before.get(bank, 0) + 1
            self.at[name] = (bank, before[bank])
        self.per, self.r = per, r

    def __getitem__(self, name):
        bank, turn = self.at[name]
        return bank, (turn if self.r is None else self.r * self.per + (turn - 2 * self.per))

    def next(self, name):
        assert self.names[self.done] == name, (self.names[self.done], name)
        self.done += 1
        return self[name]

    def ended(self):
        assert self.done == len(self.names)


def turn_names(stages):
    s1, s2, s3, s4 = (n in stages for n in (1, 2, 3, 4))
    score, turns, sums = [], [], []
    turns += ["kT", "qT0", "qT1", "qT2", "qT3"] * s2
    for s in range(UNITS + 3):
        if s2:
            score += [f"s{s}{part}" for part in "ABC"] * (s < UNITS)
            turns += [f"dT{s - 1}{h}" for h in range(2)] * (1 <= s <= UNITS)
            sums += [f"pv{s - 2}"] * (2 <= s < UNITS + 2) + [f"oT{s - 3}"] * (s >= 3)
        score += [f"x{q}" for q in range(4)] * (s3 and s == 5)
        turns += {2: ["xnT0", "xnT1"] * s1 + ["rT0", "rT1"] * s4,
                  7: ["keyT"] * s4 + ["pT0", "pT1", "pT2", "pT3"] * s3}.get(s, [])
        sums += {0: ["wo0"] * s3, 1: ["wo1"] * s3, 2: ["kx0", "kx1"] * s3, 3: ["qa0", "qb0"] * s1,
                 4: ["qx0", "qx1", "vx0"] * s3 + ["route0", "route1"] * s4, 5: ["kv0", "qa1"] * s1, 6: ["vx1"] * s3,
                 7: ["qb1"] * s1, 8: ["h0", "h1"] * s3, 9: ["kv1"] * s1, 10: ["gmean", "gvar"] * s2}.get(s, [])
    return score, turns, sums


class Round:

    BANKS = ([0, 1, 2, 3], [4, 5], [6, 7])

    def __init__(self, key, stages, used):
        self.key, self.stages, self.names = key, stages, turn_names(stages)
        self.before = [dict(u) for u in used[0]]
        self.lead = list(used[1])
        repeats = B - 3 if key == "loop" else 1
        for k, names in enumerate(self.names):
            banks = self.BANKS[k]
            assert key != "loop" or len(names) % len(banks) == 0
            for n in range(len(names)):
                bank = banks[(self.lead[k] + n) % len(banks)]
                used[0][k][bank] = used[0][k].get(bank, 0) + repeats
            used[1][k] = (self.lead[k] + repeats * len(names)) % len(banks)

    def at(self, r):
        r = r if self.key == "loop" else None
        return [Ring(self.BANKS[k], names, self.before[k], self.lead[k], len(names) // len(self.BANKS[k]), r)
                for k, names in enumerate(self.names)]

    def first(self, stage):
        return self.key == stage - 2


def all_rounds():
    used = ([{}, {}, {}], [0, 0, 0])
    stages = {-1: (1,), 0: (1, 2), 1: (1, 2, 3), "loop": (1, 2, 3, 4), B - 1: (2, 3, 4), B: (3, 4), B + 1: (4,)}
    return {key: Round(key, s, used) for key, s in stages.items()}


ROUNDS = all_rounds()

def build(nc, x, ctx, wqkv, wo, wx, wr, cols, tabs, w13, w2, out, table):
    with ExitStack() as stack:
        psum = stack.enter_context(nc.psum_tensor("psum", [P, 8, BANK], FP32))
        keys = stack.enter_context(nc.sbuf_tensor("keys", [P, B * P], FP32))
        tab = stack.enter_context(nc.sbuf_tensor("tab", [P, TAB], FP32))
        with ExitStack() as st:
            attention(nc, st, psum, x, ctx, wqkv, wo, wx, wr, cols, tabs, out, table, keys, tab)
        with ExitStack() as st:
            experts(nc, st, psum, w13, w2, out, table, keys, tab)


def alone(eng):
    eng.nop(nofuse=True)


def attention(nc, st, psum, x, ctx, wqkv, wo, wx, wr, cols, tabs, out, table, keys, tab):
    def sb(name, shape, dt=FP32):
        return st.enter_context(nc.sbuf_tensor(name, shape, dt))

    def sem(name):
        return st.enter_context(nc.semaphore(name))

    wqkv_sb = sb("wqkv_sb", [P, KC, NQKV])
    wo_sb = sb("wo_sb", [P, UNITS, D])
    wx_sb = sb("wx_sb", [P, 3, TT, T])
    wr_sb = sb("wr_sb", [P, KC, EXPERTS])
    col = sb("col", [P, COLS])
    ident = tab[:, IDENT:IDENT + P]
    ident_b = sb("ident_b", [P, P], BF16)
    tri_b = sb("tri_b", [P, 4, P], BF16)
    gnw, gnb = sb("gnw", [P, UNITS]), sb("gnb", [P, UNITS])
    half = sb("half", [P, UNITS])
    prod, dots, lam, neglam = sb("prod", [P, 2, DH]), sb("dots", [P, 2]), sb("lam", [P, 2]), sb("neglam", [P, 1])
    keycol = sb("keycol", [P, TT])

    xt, ct, xn, xn2 = (sb(n, [P, TT, D]) for n in ("xt", "ct", "xn", "xn2"))
    xnT = sb("xnT", [P, KC, T])
    rope1, rope2 = sb("rope1", [P, 2, BANK]), sb("rope2", [P, 2, BANK])
    qk = sb("qk", [P, TT, NQK])
    qT = sb("qT", [P, UNITS, T])
    kz = sb("kz", [P, 2, 4, T])
    v, v_next = sb("v", [P, TT, KV * HD]), sb("v_next", [P, TT, KV * HD])
    ex = sb("ex", [P, 2, 4, 3 * P])
    diff = sb("diff", [P, 2, 2, 3 * P])
    diffT = sb("diffT", [P, 2, 2, 3 * P])
    osc = sb("osc", [P, 2, TT, P])
    oT = sb("oT", [P, UNITS, T])
    x1 = sb("x1", [P, TT, D])
    qx, kx, vx = sb("qx", [P, 2, D]), sb("kx", [P, 2, D]), sb("vx", [P, 4, T])
    pr, prT = sb("pr", [P, 4, D]), sb("prT", [P, 4, D])
    row = sb("row", [P, TT, ROW])
    rT = sb("rT", [P, KC, T])
    st6, mv, ve, rstd = sb("st6", [P, 6, 6]), sb("mv", [P, 6, 2]), sb("ve", [P, 6]), sb("rstd", [P, 6])
    mx, nm, den, rden = (sb(n, [P, 2, 8]) for n in ("mx", "nm", "den", "rden"))
    cmul = sb("cmul", [P, 2, 4])
    go6, gmv = sb("go6", [P, UNITS, 6]), sb("gmv", [P, UNITS, 2])
    gm, gdev, gsq, gve, grs, ga, gb = (sb(n, [P, UNITS]) for n in ("gm", "gdev", "gsq", "gve", "grs", "ga", "gb"))
    mxx, nmx, denx, rdenx = (sb(n, [P, 4]) for n in ("mxx", "nmx", "denx", "rdenx"))
    rmx, rnm, rden1, rr, s8, r8 = (sb(n, [P, TT]) for n in ("rmx", "rnm", "rden1", "rr", "s8", "r8"))
    prob, rest, chosen, pexp, keyed = (sb(n, [P, TT, EXPERTS]) for n in ("prob", "rest", "chosen", "pexp", "keyed"))
    top = sb("top", [P, TT, TOPK])

    loaded = sem("loaded")
    made = sem("made")
    zeroed = sem("zeroed")
    lam_exp = sem("lam_exp")
    x_in, ctx_in, x1_load = sem("x_in"), sem("ctx_in"), sem("x1_load")
    full = [sem(f"bank{n}_full") for n in range(8)]
    free = [sem(f"bank{n}_free") for n in range(8)]
    stats, ve_in, rooted, normed = ([sem(f"{n}_{m}") for m in ("first", "later")]
                                    for n in ("stats", "ve_in", "rooted", "normed"))
    k_roped, rope_sum = sem("k_roped"), sem("rope_sum")
    v_in = sem("v_in")
    max_in, diff_in = sem("max_in"), sem("diff_in")
    gstat, groot, gdone = sem("gstat"), sem("groot"), sem("gdone")
    xmax, xrec, xnorm = sem("xmax"), sem("xrec"), sem("xnorm")
    row_in, rmax_in = sem("row_in"), sem("rmax_in")
    out_done, row_done = sem("out_done"), sem("row_done")
    step = [None] + [sem(f"step{n}") for n in range(1, 5)]


    def begin(eng, ring, name):
        bank, turn = ring.next(name)
        eng.wait_ge(free[bank], turn)
        return psum[:, bank, :], full[bank]

    def filled(eng, ring, name):
        bank, turn = ring[name]
        eng.wait_ge(full[bank], turn)
        return psum[:, bank, :], free[bank]

    def emptied(eng, ring, name):
        bank, turn = ring[name]
        eng.wait_ge(free[bank], turn + 1)

    def rounds(fori, body):
        for r in range(-1, 2):
            body(r, ROUNDS[r])
        with fori(2, B - 1) as r:
            body(r, ROUNDS["loop"])
        for r in range(B - 1, B + 2):
            body(r, ROUNDS[r])

    block_context = nc.Block()
    block = block_context.__enter__()

    @block.sync
    def _(sp):
        def rows_of(a, i):
            return a[bass.ds(i * T, T), :].rearrange("(t p) d -> p t d", p=P)

        sp.dma_start(tab[:, :], tabs).then_inc(loaded, 16)
        sp.dma_start(xt[:, :, :], rows_of(x, 0)).then_inc(x_in, 16)
        for dst, src in ((col[:, :], cols), (wqkv_sb[:, :, :], wqkv), (wx_sb[:, :, :, :], wx),
                         (wo_sb[:, :, :], wo), (wr_sb[:, :, :], wr)):
            sp.dma_start(dst, src).then_inc(loaded, 16)
        sp.dma_start(ct[:, :, :], rows_of(ctx, 0)).then_inc(ctx_in, 16)

        def body(r, rd, more=True):
            score, turns, sums = rd.at(r)
            if 3 in rd.stages:
                b = r - 1
                if not rd.first(3):
                    sp.wait_ge(out_done, 16 * b)
                    alone(sp)
                    sp.wait_ge(normed[1], 2 * TT * b)
                    alone(sp)
                sp.dma_start(x1[:, :, :], rows_of(x, b)).then_inc(x1_load, 16)
            if 1 in rd.stages and more:
                sp.wait_ge(normed[0], TT * (r + 2))
                alone(sp)
                sp.dma_start(xt[:, :, :], rows_of(x, r + 2)).then_inc(x_in, 16)
            if 3 in rd.stages and 2 in rd.stages:
                bank, turn = sums["vx1"]
                sp.wait_ge(full[bank], turn)
                alone(sp)
                sp.dma_start(ct[:, :, :], rows_of(ctx, r)).then_inc(ctx_in, 16)
            if 4 in rd.stages:
                sp.wait_ge(row_in, r - 1)
                alone(sp)
                sp.dma_start(rows_of(table, r - 2), row[:, :, :]).then_inc(row_done, 16)
            if 3 in rd.stages:
                emptied(sp, sums, "h1")
                alone(sp)
                sp.dma_start(rows_of(out, r - 1), x1[:, :, :]).then_inc(out_done, 16)

        for r in range(-1, 2):
            body(r, ROUNDS[r])
        with nc.sync.Fori(2, B - 2) as r:
            body(r, ROUNDS["loop"])
        body(B - 2, ROUNDS["loop"], more=False)
        for r in range(B - 1, B + 2):
            body(r, ROUNDS[r])
        sp.wait_ge(out_done, 16 * B)
        sp.wait_ge(row_done, 16 * B)

    @block.gpsimd
    def _(pool):
        nc.gpsimd.memset(half[:, :], -0.5).then_inc(zeroed, 1)
        nc.gpsimd.memset(kz[:, :, :, :], 0.0).then_inc(zeroed, 1)
        pool.wait_ge(zeroed, 2)

        def body(r, rd):
            score, turns, sums = rd.at(r)
            s1, s2, s3 = (n in rd.stages for n in (1, 2, 3))

            def root(later, b, n):
                k, per = 2 * later + n, (2 * TT if later else TT)
                pool.wait_ge(stats[later], b * per + (n + 1))
                alone(pool)
                nc.gpsimd.tensor_scalar(ve[:, k:k + 1], mv[:, k, 1:2], EPS, None, ALU.add).then_inc(ve_in[later], 1)
                pool.wait_ge(ve_in[later], b * per + (n + 1))
                nc.gpsimd.tensor_tensor(rstd[:, k:k + 1], ve[:, k:k + 1], half[:, 0:1], ALU.pow).then_inc(rooted[later], 1)

            def rope(k):
                lo, n = ROPE_PARTS[k % 3]
                if k % 3 < 2:
                    emptied(pool, sums, ("qa", "qb")[k % 3] + str(k // 3))
                else:
                    pool.wait_ge(k_roped, (r + 1) * TT + (k // 3 + 1))
                nc.gpsimd.tensor_tensor(qk[:, k // 3, lo:lo + n], rope1[:, k % 2, 0:n], rope2[:, k % 2, 0:n],
                                        ALU.add).then_inc(rope_sum, 1)

            if s1:
                root(0, r + 1, 0)
                root(0, r + 1, 1)
            if s3:
                root(1, r - 1, 0)
                root(1, r - 1, 1)
            if s1:
                for k in range(4):
                    rope(k)
            if s3:
                for q in range(4):
                    pool.wait_ge(xrec, (r - 1) * 4 + (q + 1))
                    alone(pool)
                    nc.gpsimd.tensor_scalar(pr[:, q, :], pr[:, q, :], rdenx[:, q:q + 1], None, ALU.mult).then_inc(xnorm, 1)
            if s1:
                rope(4)
            if s3:
                root(1, r - 1, 2)
                root(1, r - 1, 3)
            if s1:
                rope(5)
            if s2:
                emptied(pool, sums, "gvar")
                nc.gpsimd.tensor_tensor(grs[:, :], gve[:, :], half[:, :], ALU.pow).then_inc(groot, 1)
            if s1:
                emptied(pool, sums, "kv0")
                emptied(pool, sums, "kv1")
                if s2:
                    filled(pool, sums, f"pv{UNITS - 1}")
                alone(pool)
                nc.gpsimd.tensor_copy(v[:, :, :], v_next[:, :, :]).then_inc(v_in, 1)

        rounds(nc.gpsimd.Fori, body)

    @block.scalar
    def _(act):
        act.wait_ge(made, 3)
        nc.scalar.activation(lam[:, :], dots[:, :], ACT.Exp).then_inc(lam_exp, 1)

        def body(r, rd):
            score, turns, sums = rd.at(r)
            s1, s2, s3, s4 = (n in rd.stages for n in (1, 2, 3, 4))

            def exponentials(j):
                act.wait_ge(max_in, r * UNITS + (j + 1))
                for t in range(TT):
                    for q in range(4):
                        bank, _ = score[f"s{j}" + ("A" if t == 0 else "BC"[q // 2])]
                        lo, n = (q * P, P) if t == 0 else (q % 2 * T, T)
                        k = 4 * t + q
                        ins = nc.scalar.activation(ex[:, j % 2, q, t * P:t * P + n], psum[:, bank, lo:lo + n], ACT.Exp,
                                                   bias=nm[:, j % 2, k:k + 1], scale=SCALE,
                                                   accum_out=den[:, j % 2, k:k + 1])
                        if q == 3 or (t == 1 and q == 1):
                            ins.then_inc(free[bank], 1)

            def turned(j):
                for h in range(2):
                    ps, freed = filled(act, turns, f"dT{j}{h}")
                    nc.scalar.copy(diffT[:, j % 2, h, :], ps[:, 0:3 * P]).then_inc(freed, 1)

            def unit(s):
                if s2 and s < UNITS:
                    exponentials(s)
                if s2 and 1 <= s <= UNITS:
                    turned(s - 1)

            def value(t):
                ps, freed = filled(act, sums, f"kv{t}")
                act.wait_ge(k_roped, (r + 1) * TT + (t + 1))
                nc.scalar.copy(v_next[:, t, :], ps[:, 256:512]).then_inc(freed, 1)

            def halves(ring, name, dst):
                ps, freed = filled(act, ring, name)
                nc.scalar.copy(dst, ps.rearrange("p (a b) -> p a b", a=dst.shape[1])).then_inc(freed, 1)

            if s2:
                for n in range(4):
                    halves(turns, f"qT{n}", qT[:, 2 * n:2 * n + 2, :])
            unit(0)
            unit(1)
            unit(2)
            if s3:
                for n in range(2):
                    ps, freed = filled(act, sums, f"kx{n}")
                    nc.scalar.activation(kx[:, n, :], ps, ACT.Identity, bias=col[:, KB + n:KB + n + 1]).then_inc(freed, 1)
            unit(3)
            unit(4)
            if s3:
                for n in range(2):
                    ps, freed = filled(act, sums, f"qx{n}")
                    nc.scalar.activation(qx[:, n, :], ps, ACT.Identity, bias=col[:, QB + n:QB + n + 1]).then_inc(freed, 1)
                halves(sums, "vx0", vx[:, 0:2, :])
            if s4:
                for t in range(TT):
                    act.wait_ge(rmax_in, (r - 2) * TT + (t + 1))
                    bank, _ = sums[f"route{t}"]
                    nc.scalar.activation(pexp[:, t, :], psum[:, bank, 0:EXPERTS], ACT.Exp, bias=rnm[:, t:t + 1],
                                         scale=1.0, accum_out=rden1[:, t:t + 1]).then_inc(free[bank], 1)
            unit(5)
            if s3:
                for q in range(4):
                    act.wait_ge(xmax, (r - 1) * 4 + (q + 1))
                    bank, _ = score[f"x{q}"]
                    nc.scalar.activation(pr[:, q, :], psum[:, bank, :], ACT.Exp, bias=nmx[:, q:q + 1], scale=1.0,
                                         accum_out=denx[:, q:q + 1]).then_inc(free[bank], 1)
            if s1:
                value(0)
            unit(6)
            if s3:
                halves(sums, "vx1", vx[:, 2:4, :])
            unit(7)
            if s3:
                for q in (0, 2):
                    halves(turns, f"pT{q}", prT[:, :, q * P:(q + 1) * P])
            unit(8)
            if s1:
                value(1)

        rounds(nc.scalar.Fori, body)

    @block.vector
    def _(dve):
        vec = nc.vector
        dve.wait_ge(loaded, 16 * 6)
        vec.tensor_tensor(prod[:, 0, :], col[:, LAM:LAM + DH], col[:, LAM + DH:LAM + 2 * DH], ALU.mult)
        vec.tensor_tensor(prod[:, 1, :], col[:, LAM + 2 * DH:LAM + 3 * DH], col[:, LAM + 3 * DH:LAM + 4 * DH],
                          ALU.mult).then_inc(made, 1)
        vec.tensor_scalar(gnw[:, :], col[:, GW:GW + UNITS], 1.0 - LAMBDA_INIT, None, ALU.mult)
        vec.tensor_scalar(gnb[:, :], col[:, GB:GB + UNITS], 1.0 - LAMBDA_INIT, None, ALU.mult)
        vec.tensor_copy(ident_b[:, :], ident)
        vec.tensor_copy(tri_b[:, :, :], tab[:, TRI:TRI + 4 * P].rearrange("p (a b) -> p a b", a=4)).then_inc(made, 1)
        dve.wait_ge(made, 2)
        vec.tensor_reduce(dots[:, :], prod[:, :, :], AX.X, ALU.add).then_inc(made, 1)
        vec.tensor_copy(keycol[:, :], tab[:, KEY0:KEY0 + TT]).then_inc(made, 1)
        dve.wait_ge(lam_exp, 1)
        vec.scalar_tensor_tensor(out=neglam[:, :], in0=lam[:, 1:2], scalar=LAMBDA_INIT, in1=lam[:, 0:1],
                                 op0=ALU.subtract, op1=ALU.subtract).then_inc(made, 1)
        dve.wait_ge(made, 5)
        dve.wait_ge(zeroed, 2)

        def body(r, rd):
            score, turns, sums = rd.at(r)
            s1, s2, s3, s4 = (n in rd.stages for n in (1, 2, 3, 4))
            batch = [None, r + 1, r, r - 1, r - 2]
            steps = [0] * 5

            def after(stage, ins):
                steps[stage] += 1
                ins.then_inc(step[stage], 1)
                dve.wait_ge(step[stage], batch[stage] * STEPS[stage] + steps[stage])

            def measure(later, n, src):
                k = 2 * later + n
                after(3 if later else 1, vec.bn_stats(st6[:, k, :], src))
                alone(dve)
                vec.bn_aggr(mv[:, k, :], st6[:, k, :]).then_inc(stats[later], 1)

            def normalise(later, n, src, dst):
                k, per = 2 * later + n, (2 * TT if later else TT)
                dve.wait_ge(rooted[later], batch[3 if later else 1] * per + (n + 1))
                vec.tensor_scalar(dst, src, mv[:, k, 0:1], rstd[:, k:k + 1], ALU.subtract, ALU.mult).then_inc(normed[later], 1)

            def halves(ring, name, dst):
                ps, freed = filled(dve, ring, name)
                vec.tensor_copy(dst, ps.rearrange("p (a b) -> p a b", a=dst.shape[1])).then_inc(freed, 1)

            def rope(k):
                t, part = divmod(k, 3)
                ps, freed = filled(dve, sums, ("qa", "qb", "kv")[part] + str(t))
                if k >= 2:
                    dve.wait_ge(rope_sum, (r + 1) * (3 * TT) + (k - 1))
                n = ROPE_PARTS[part][1]
                g, h = n // DH, DH // 2
                src = ps[:, 0:n].rearrange("p (g d) -> p g d", d=DH)
                a = rope1[:, k % 2, 0:n].rearrange("p (g d) -> p g d", d=DH)
                b = rope2[:, k % 2, 0:n].rearrange("p (g d) -> p g d", d=DH)
                cos = tab[:, COS + t * DH:COS + (t + 1) * DH]
                sin = tab[:, SIN + t * DH:SIN + (t + 1) * DH]
                vec.tensor_tensor(b[:, :, 0:h], src[:, :, h:DH], sin[:, 0:h].unsqueeze(1).broadcast_to([P, g, h]), ALU.mult)
                vec.tensor_tensor(b[:, :, h:DH], src[:, :, 0:h], sin[:, h:DH].unsqueeze(1).broadcast_to([P, g, h]), ALU.mult)
                ins = vec.tensor_tensor(a, src, cos.unsqueeze(1).broadcast_to([P, g, DH]), ALU.mult)
                ins.then_inc(freed if part < 2 else k_roped, 1)

            def maxima(j):
                for part, at in zip("ABC", (0, 4, 6)):
                    ps, _ = filled(dve, score, f"s{j}{part}")
                    n = 4 if part == "A" else 2
                    ins = vec.tensor_reduce(mx[:, j % 2, at:at + n], ps.rearrange("p (a b) -> p a b", a=n), AX.X, ALU.max)
                after(2, ins)
                vec.tensor_scalar(nm[:, j % 2, :], mx[:, j % 2, :], -SCALE, None, ALU.mult).then_inc(max_in, 1)

            def difference(j):
                if j >= 2:
                    emptied(dve, sums, f"pv{j - 2}")
                emptied(dve, score, f"s{j}C")
                after(2, vec.reciprocal(rden[:, j % 2, :], den[:, j % 2, :]))
                d = den[:, j % 2, :].rearrange("p (a i) -> p a i", i=2)
                rd_ = rden[:, j % 2, :].rearrange("p (a i) -> p a i", i=2)
                after(2, vec.scalar_tensor_tensor(out=cmul[:, j % 2, :], in0=rd_[:, :, 1], scalar=neglam[:, 0:1],
                                                  in1=d[:, :, 0], op0=ALU.mult, op1=ALU.mult))
                for t in range(TT):
                    for h in range(2):
                        s = slice(t * P, P + 2 * t * P)
                        ins = vec.scalar_tensor_tensor(out=diff[:, j % 2, h, s], in0=ex[:, j % 2, 2 * h + 1, s],
                                                       scalar=cmul[:, j % 2, 2 * t + h:2 * t + h + 1],
                                                       in1=ex[:, j % 2, 2 * h, s], op0=ALU.mult, op1=ALU.add)
                ins.then_inc(diff_in, 1)

            def scaled(j):
                ps, freed = filled(dve, sums, f"pv{j}")
                r1 = rden[:, j % 2, :].rearrange("p (a i) -> p a i", i=2)[:, :, 0:1].broadcast_to([P, 4, HD])
                vec.tensor_tensor(osc[:, j % 2, :, :].rearrange("p t (h d) -> p (t h) d", h=2),
                                  ps[:, 0:T].rearrange("p (a d) -> p a d", d=HD), r1, ALU.mult).then_inc(freed, 1)

            def collected(j):
                ps, freed = filled(dve, sums, f"oT{j}")
                vec.bn_stats(go6[:, j, :], ps[:, 0:T])
                vec.tensor_copy(oT[:, j, :], ps[:, 0:T]).then_inc(freed, 1)

            def unit(s, other=None):
                if s2 and 1 <= s <= UNITS:
                    difference(s - 1)
                if other:
                    other()
                if not s2:
                    return
                if s < UNITS:
                    maxima(s)
                if 2 <= s < UNITS + 2:
                    scaled(s - 2)
                if 3 <= s:
                    collected(s - 3)

            def residual(t):
                if t == 0:
                    dve.wait_ge(x1_load, r * 16)
                ps, freed = filled(dve, sums, f"wo{t}")
                vec.tensor_tensor(x1[:, t, :], x1[:, t, :], ps, ALU.add).then_inc(freed, 1)
                emptied(dve, sums, f"wo{t}")
                measure(1, t, x1[:, t, :])

            def choose():
                emptied(dve, sums, "route0")
                emptied(dve, sums, "route1")
                after(4, vec.reciprocal(rr[:, :], rden1[:, :]))
                vec.tensor_scalar(prob[:, 0, :], pexp[:, 0, :], rr[:, 0:1], None, ALU.mult)
                after(4, vec.tensor_scalar(prob[:, 1, :], pexp[:, 1, :], rr[:, 1:2], None, ALU.mult))
                alone(dve)
                vec.max(top[:, 0, :], prob[:, 0, :])
                after(4, vec.max(top[:, 1, :], prob[:, 1, :]))
                after(4, vec.tensor_reduce(s8[:, :], top[:, :, :], AX.X, ALU.add))
                vec.reciprocal(r8[:, :], s8[:, :])
                vec.match_replace(rest[:, 0, :], top[:, 0, :], prob[:, 0, :], -1.0)
                after(4, vec.match_replace(rest[:, 1, :], top[:, 1, :], prob[:, 1, :], -1.0))
                after(4, vec.tensor_scalar(chosen[:, :, :], rest[:, :, :], 0.0, None, ALU.is_lt))
                for t in range(TT):
                    vec.tensor_scalar(keyed[:, t, :], chosen[:, t, :], keycol[:, t:t + 1], None, ALU.mult)
                    ins = vec.scalar_tensor_tensor(out=row[:, t, D:ROW], in0=prob[:, t, :], scalar=r8[:, t:t + 1],
                                                   in1=chosen[:, t, :], op0=ALU.mult, op1=ALU.mult)
                ins.then_inc(row_in, 1)

            if s2:
                ps, freed = filled(dve, turns, "kT")
                for q in range(4):
                    rows = slice(DH * q, DH * q + DH)
                    ins = vec.tensor_copy(kz[rows, :, q, :], ps[rows, :].rearrange("p (a b) -> p a b", a=2))
                ins.then_inc(freed, 1)
            if s1:
                dve.wait_ge(x_in, (r + 1) * 16 + 16)
                for t in range(TT):
                    measure(0, t, xt[:, t, :])
            unit(0)

            def gap0():
                if s1:
                    for t in range(TT):
                        normalise(0, t, xt[:, t, :], xn[:, t, :])
                if s3:
                    residual(0)

            def gap1():
                if s3:
                    residual(1)
                    normalise(1, 0, x1[:, 0, :], xn2[:, 0, :])

            def gap2():
                if s1:
                    halves(turns, "xnT0", xnT[:, 0:2, :])
                    halves(turns, "xnT1", xnT[:, 2:4, :])
                if s3:
                    normalise(1, 1, x1[:, 1, :], xn2[:, 1, :])
                if s4:
                    halves(turns, "rT0", rT[:, 0:2, :])
                    halves(turns, "rT1", rT[:, 2:4, :])

            def gap3():
                if s1:
                    rope(0)
                    rope(1)

            def gap4():
                if s4:
                    for t in range(TT):
                        ps, _ = filled(dve, sums, f"route{t}")
                        after(4, vec.tensor_reduce(rmx[:, t:t + 1], ps[:, 0:EXPERTS], AX.X, ALU.max))
                        vec.tensor_scalar(rnm[:, t:t + 1], rmx[:, t:t + 1], -1.0, None, ALU.mult).then_inc(rmax_in, 1)

            def gap5():
                if s3:
                    for q in range(4):
                        ps, _ = filled(dve, score, f"x{q}")
                        after(3, vec.tensor_reduce(mxx[:, q:q + 1], ps, AX.X, ALU.max))
                        vec.tensor_scalar(nmx[:, q:q + 1], mxx[:, q:q + 1], -1.0, None, ALU.mult).then_inc(xmax, 1)
                if s1:
                    rope(2)
                    rope(3)

            def gap6():
                if s3:
                    for q in range(4):
                        emptied(dve, score, f"x{q}")
                        vec.reciprocal(rdenx[:, q:q + 1], denx[:, q:q + 1]).then_inc(xrec, 1)
                if s4:
                    choose()

            def gap7():
                if s4:
                    ps, freed = filled(dve, turns, "keyT")
                    after(4, vec.tensor_scalar(keycol[:, :], keycol[:, :], -1.0, None, ALU.add))
                    alone(dve)
                    vec.tensor_copy(keys[:, bass.ds((r - 2) * P, P)], ps[:, 0:P]).then_inc(freed, 1)
                if s1:
                    rope(4)
                if s3:
                    for q in (1, 3):
                        halves(turns, f"pT{q}", prT[:, :, q * P:(q + 1) * P])

            def gap8():
                if s3:
                    for t in range(TT):
                        ps, freed = filled(dve, sums, f"h{t}")
                        vec.scalar_tensor_tensor(out=x1[:, t, :], in0=ps, scalar=col[:, VB + t:VB + t + 1],
                                                 in1=x1[:, t, :], op0=ALU.add, op1=ALU.add).then_inc(freed, 1)
                        emptied(dve, sums, f"h{t}")
                        measure(1, TT + t, x1[:, t, :])

            def gap9():
                if s1:
                    rope(5)
                if s3:
                    if not rd.first(3):
                        dve.wait_ge(row_done, (r - 1) * 16)
                    for t in range(TT):
                        normalise(1, TT + t, x1[:, t, :], row[:, t, 0:D])

            for s, other in enumerate((gap0, gap1, gap2, gap3, gap4, gap5, gap6, gap7, gap8, gap9)):
                unit(s + 1, other)
            if s2:
                emptied(dve, sums, f"oT{UNITS - 1}")
                alone(dve)
                for j in range(UNITS):
                    ins = vec.bn_aggr(gmv[:, j, :], go6[:, j, :])
                ins.then_inc(gstat, 1)
                ps, freed = filled(dve, sums, "gmean")
                after(2, vec.tensor_copy(gm[:, :], ps[:, 0:UNITS]))
                after(2, vec.tensor_tensor(gdev[:, :], gmv[:, :, 0], gm[:, :], ALU.subtract))
                after(2, vec.tensor_tensor(gsq[:, :], gdev[:, :], gdev[:, :], ALU.mult))
                vec.tensor_tensor(gdev[:, :], gsq[:, :], gmv[:, :, 1], ALU.add).then_inc(freed, 1)
                ps, freed = filled(dve, sums, "gvar")
                vec.tensor_scalar(gve[:, :], ps[:, 0:UNITS], EPS, None, ALU.add).then_inc(freed, 1)
                dve.wait_ge(groot, r + 1)
                after(2, vec.tensor_tensor(ga[:, :], grs[:, :], gnw[:, :], ALU.mult))
                after(2, vec.tensor_tensor(gsq[:, :], gm[:, :], ga[:, :], ALU.mult))
                after(2, vec.tensor_tensor(gb[:, :], gnb[:, :], gsq[:, :], ALU.subtract))
                for j in range(UNITS):
                    ins = vec.tensor_scalar(oT[:, j, :], oT[:, j, :], ga[:, j:j + 1], gb[:, j:j + 1], ALU.mult, ALU.add)
                ins.then_inc(gdone, 1)
            for n in rd.stages:
                assert steps[n] == STEPS[n], (n, steps)

        rounds(nc.vector.Fori, body)

    @block.tensor
    def _(pe):
        for n in range(8):
            pe.sem_inc(free[n], 1)
        pe.wait_ge(loaded, 16 * 6)
        pe.wait_ge(made, 2)

        def mm(out_, lhsT, rhs, start, stop):
            return nc.tensor.matmul(out_, lhsT, rhs, start=start, stop=stop)

        def body(r, rd):
            score, turns, sums = rd.at(r)
            s1, s2, s3, s4 = (n in rd.stages for n in (1, 2, 3, 4))

            def turn(name, pieces):
                ps, done = begin(pe, turns, name)
                for n, piece in enumerate(pieces):
                    ins = nc.tensor.transpose(ps[:, n * P:(n + 1) * P], piece, ident)
                ins.then_inc(done, 1)

            def product(name, groups, n=BANK):
                ps, done = begin(pe, sums, name)
                for g, pairs in enumerate(groups):
                    for k, (lhsT, rhs) in enumerate(pairs):
                        ins = mm(ps[:, g * n:(g + 1) * n], lhsT, rhs, k == 0, k == len(pairs) - 1)
                ins.then_inc(done, 1)

            def scores(j):
                g = j // 4
                if j % 2 == 0:
                    emptied(pe, turns, f"qT{j // 2}")
                ps, done = begin(pe, score, f"s{j}A")
                mm(ps, qT[:, j, 0:P], kz[:, g, :, 0:P], True, False)
                mm(ps, ident_b[:, :], tri_b[:, :, :], False, True).then_inc(done, 1)
                for k, part in enumerate("BC"):
                    ps, done = begin(pe, score, f"s{j}{part}")
                    mm(ps, qT[:, j, P:2 * P], kz[:, g, 2 * k:2 * k + 2, :], True, False)
                    mm(ps.rearrange("p (a b) -> p a b", a=2)[:, :, P:2 * P], ident_b[:, :], tri_b[:, 0:2, :],
                       False, True).then_inc(done, 1)

            def turn_difference(j):
                pe.wait_ge(diff_in, r * UNITS + (j + 1))
                for h in range(2):
                    turn(f"dT{j}{h}", [diff[:, j % 2, h, n * P:(n + 1) * P] for n in range(3)])

            def weigh(j):
                if j == 0:
                    pe.wait_ge(v_in, r + 1)
                emptied(pe, turns, f"dT{j}0")
                emptied(pe, turns, f"dT{j}1")
                ps, done = begin(pe, sums, f"pv{j}")
                for h in range(2):
                    vh = v[:, :, (2 * (j // 4) + h) * HD:(2 * (j // 4) + h + 1) * HD]
                    dT = diffT[:, j % 2, h, :]
                    mm(ps[:, h * HD:(h + 1) * HD], dT[:, 0:P], vh[:, 0, :], True, True)
                    mm(ps[:, P + h * HD:P + (h + 1) * HD], dT[:, P:2 * P], vh[:, 0, :], True, False)
                    ins = mm(ps[:, P + h * HD:P + (h + 1) * HD], dT[:, 2 * P:3 * P], vh[:, 1, :], False, True)
                ins.then_inc(done, 1)

            def turn_output(j):
                emptied(pe, sums, f"pv{j}")
                ps, done = begin(pe, sums, f"oT{j}")
                for t in range(TT):
                    ins = nc.tensor.transpose(ps[:, t * P:(t + 1) * P], osc[:, j % 2, t, :], ident)
                ins.then_inc(done, 1)

            def unit(s):
                if not s2:
                    return
                if s < UNITS:
                    scores(s)
                if 1 <= s <= UNITS:
                    turn_difference(s - 1)
                if 2 <= s < UNITS + 2:
                    weigh(s - 2)
                if 3 <= s:
                    turn_output(s - 3)

            def output(t):
                product(f"wo{t}", [[(oT[:, j, t * P:(t + 1) * P], wo_sb[:, j, :]) for j in range(UNITS)]])

            def qkv(t, part):
                product(("qa", "qb", "kv")[part] + str(t),
                        [[(xnT[:, c, t * P:(t + 1) * P], wqkv_sb[:, c, part * BANK:(part + 1) * BANK]) for c in range(KC)]])

            def context_v(n):
                product(f"vx{n}", [[(ct[:, t, lt * P:(lt + 1) * P], wx_sb[:, 2, t, :]) for t in range(TT)]
                                   for lt in (2 * n, 2 * n + 1)], T)

            if s2:
                pe.wait_ge(rope_sum, (r + 1) * (3 * TT))
                turn("kT", [qk[:, t, (UNITS + g) * P:(UNITS + g + 1) * P] for g in range(2) for t in range(TT)])
                for n in range(4):
                    turn(f"qT{n}", [qk[:, t, j * P:(j + 1) * P] for j in (2 * n, 2 * n + 1) for t in range(TT)])
                emptied(pe, turns, "kT")
            unit(0)
            if s3:
                pe.wait_ge(gdone, r)
                output(0)
            unit(1)
            if s3:
                output(1)
            unit(2)
            if s1:
                pe.wait_ge(normed[0], (r + 2) * TT)
                for n in range(2):
                    turn(f"xnT{n}", [xn[:, t, c * P:(c + 1) * P] for c in (2 * n, 2 * n + 1) for t in range(TT)])
            if s4:
                pe.wait_ge(normed[1], (r - 1) * (2 * TT))
                for n in range(2):
                    turn(f"rT{n}", [row[:, t, c * P:(c + 1) * P] for c in (2 * n, 2 * n + 1) for t in range(TT)])
            if s3:
                pe.wait_ge(ctx_in, r * 16)
                for n in range(2):
                    product(f"kx{n}", [[(wx_sb[:, 1, t, n * P:(n + 1) * P], ct[:, t, :]) for t in range(TT)]])
            unit(3)
            if s1:
                emptied(pe, turns, "xnT0")
                emptied(pe, turns, "xnT1")
                qkv(0, 0)
                qkv(0, 1)
            unit(4)
            if s3:
                pe.wait_ge(normed[1], (r - 1) * (2 * TT) + TT)
                for n in range(2):
                    product(f"qx{n}", [[(wx_sb[:, 0, t, n * P:(n + 1) * P], xn2[:, t, :]) for t in range(TT)]])
                context_v(0)
            if s4:
                emptied(pe, turns, "rT0")
                emptied(pe, turns, "rT1")
                for t in range(TT):
                    product(f"route{t}", [[(rT[:, c, t * P:(t + 1) * P], wr_sb[:, c, :]) for c in range(KC)]], EXPERTS)
            unit(5)
            if s3:
                for name in ("kx0", "kx1", "qx0", "qx1"):
                    emptied(pe, sums, name)
                for q in range(4):
                    ps, done = begin(pe, score, f"x{q}")
                    mm(ps, qx[:, 0, q * P:(q + 1) * P], kx[:, 0, :], True, False)
                    mm(ps, qx[:, 1, q * P:(q + 1) * P], kx[:, 1, :], False, True).then_inc(done, 1)
            if s1:
                qkv(0, 2)
                qkv(1, 0)
            unit(6)
            if s3:
                context_v(1)
            unit(7)
            if s4:
                pe.wait_ge(row_in, r - 1)
                turn("keyT", [keyed[:, :, :].rearrange("p a b -> p (a b)")])
            if s1:
                qkv(1, 1)
            if s3:
                for q in range(4):
                    pe.wait_ge(xnorm, (r - 1) * 4 + (q + 1))
                    turn(f"pT{q}", [pr[:, q, k * P:(k + 1) * P] for k in range(4)])
            unit(8)
            if s3:
                emptied(pe, turns, "pT2")
                emptied(pe, turns, "pT3")
                emptied(pe, sums, "vx0")
                emptied(pe, sums, "vx1")
                for n in range(2):
                    product(f"h{n}", [[(vx[:, k, n * P:(n + 1) * P], prT[:, k, :]) for k in range(4)]])
            unit(9)
            if s1:
                qkv(1, 2)
            unit(10)
            if s2:
                heads = tab[:, HEADS:HEADS + P]
                pe.wait_ge(gstat, r + 1)
                product("gmean", [[(heads, gmv[:, :, 0])]], UNITS)
                emptied(pe, sums, "gmean")
                product("gvar", [[(heads, gdev[:, :])]], UNITS)
            for ring in (score, turns, sums):
                ring.ended()

        rounds(nc.tensor.Fori, body)

    block_context.__exit__(None, None, None)


def experts(nc, st, psum, w13, w2, out, table, keys, tab):
    def sb(name, shape, dt=FP32):
        return st.enter_context(nc.sbuf_tensor(name, shape, dt))

    def sem(name):
        return st.enter_context(nc.semaphore(name))

    SLOTS = 4
    w13_sb = [sb(f"w13_sb{n}", [P, KC, 2 * FF]) for n in range(SLOTS)]
    w2a_sb = [sb(f"w2a_sb{n}", [P, D]) for n in range(SLOTS)]
    w2b_sb = [sb(f"w2b_sb{n}", [FF - P, D]) for n in range(SLOTS)]
    ident = tab[:, IDENT:IDENT + P]
    firsts = sb("firsts", [P, CAP])
    both = sb("both", [EXPERTS, 2 * CAP])
    slot = sb("slot", [EXPERTS, CAP])
    sloti, low, high = (sb(n, [EXPERTS, CAP], I32) for n in ("sloti", "low", "high"))
    held = sb("held", [EXPERTS, CAP])
    rowf = sb("rowf", [EXPERTS, 2, CAP])
    tmp, rows_to = sb("tmp", [EXPERTS, CAP]), sb("rows_to", [EXPERTS, CAP])
    from_idx = sb("from_idx", [P, PAIRS], I32)
    to_idx = sb("to_idx", [CAP, EXPERTS], I32)
    gidx = [sb(f"gidx{n}", [P, 1], I32) for n in range(2)]
    sidx = [sb(f"sidx{n}", [CAP, 1], I32) for n in range(2)]
    gx = [sb(f"gx{n}", [P, ROW]) for n in range(2)]
    wcol = [sb(f"wcol{n}", [P, 1]) for n in range(2)]
    gxT = [sb(f"gxT{n}", [P, KC, P]) for n in range(2)]
    eh, sig, gate = sb("eh", [P, FF]), sb("sig", [P, FF]), sb("gate", [P, FF])
    g = [sb(f"g{n}", [P, FF]) for n in range(2)]
    gT = [sb(f"gT{n}", [P, 2, P]) for n in range(2)]
    y = [sb(f"y{n}", [P, D]) for n in range(2)]
    zeros = sb("zeros", [CAP, D])

    pick, joined = sem("pick"), sem("joined")
    picked_out, rows_in, index_in = sem("picked_out"), sem("rows_in"), sem("index_in")
    zero_in, zero_out = sem("zero_in"), sem("zero_out")
    w_in = [sem(f"w_in{n}") for n in range(SLOTS)]
    idx_in, sidx_in, added = sem("idx_in"), sem("sidx_in"), sem("added")
    gx_in = [sem(f"gx_in{n}") for n in range(2)]
    gx_turned, gxT_in, wcol_in = sem("gx_turned"), sem("gxT_in"), sem("wcol_in")
    hidden, eh_in, g_in, g_turned, gT_in, y_full, y_in = (
        sem(n) for n in ("hidden", "eh_in", "g_in", "g_turned", "gT_in", "y_full", "y_in"))
    moe_step = sem("moe_step")

    turn_ps = [psum[:, n, :] for n in range(2)]
    hidden_ps = [psum[:, 2 + n, 0:2 * FF] for n in range(2)]
    gate_ps = [psum[:, 4 + n, 0:2 * P] for n in range(2)]
    y_ps = [psum[:, 6 + n, :] for n in range(2)]

    with nc.Block() as block:
        @block.sync
        def _(sp):
            def weights(e, n):
                sp.dma_start(w13_sb[n][:, :, :], w13[bass.ds(e * P, P), :].rearrange("p (c f) -> p c f", c=KC)).then_inc(w_in[n], 16)
                sp.dma_start(w2a_sb[n][:, :], w2[bass.ds(e * FF, P), :]).then_inc(w_in[n], 16)
                sp.dma_start(w2b_sb[n][:, :], w2[bass.ds(e * FF + P, FF - P), :]).then_inc(w_in[n], 16)

            for n in range(SLOTS):
                weights(n, n)
            sp.wait_ge(zero_in, 1)
            sp.dma_start(out[TOKENS:TOKENS + CAP, :], zeros[:, :]).then_inc(zero_out, 16)
            sp.wait_ge(pick, 8)
            sp.dma_start(both[:, 0:CAP], firsts[0:EXPERTS, :]).then_inc(joined, 16)
            sp.dma_start(both[:, CAP:2 * CAP], firsts[EXPERTS:P, :]).then_inc(joined, 16)
            with nc.sync.Fori(0, EXPERTS // SLOTS - 1) as i:
                for n in range(SLOTS):
                    sp.wait_ge(y_full, i * 2 + (n // 2 + 1))
                    weights(i * SLOTS + (SLOTS + n), n)

        @block.gpsimd
        def _(pool):
            nc.gpsimd.memset(zeros[:, :], 0.0).then_inc(zero_in, 1)
            pool.wait_ge(zero_out, 16)
            pool.wait_ge(index_in, 2)

            def fetch(k, n):
                nc.gpsimd.tensor_copy(gidx[n][:, :], from_idx[:, bass.ds(k, 1)]).then_inc(idx_in, 1)
                pool.wait_ge(idx_in, k + 1)
                alone(pool)
                nc.gpsimd.indirect_dma_start(
                    out=gx[n][:, :], out_offset=None, in_=table,
                    in_offset=bass.IndirectOffsetOnAxis(ap=gidx[n][:, 0:1], axis=0)).then_inc(gx_in[n], 16)

            def add(i, n):
                k = 2 * i + n
                pool.wait_ge(y_in, k + 1)
                alone(pool)
                for h in range(2):
                    nc.gpsimd.tensor_copy(sidx[h][:, :], to_idx[:, bass.ds(2 * k + h, 1)]).then_inc(sidx_in, 1)
                for h in range(2):
                    pool.wait_ge(sidx_in, 2 * k + 2)
                    if h:
                        pool.wait_ge(added, 32 * k + 16)
                    alone(pool)
                    nc.gpsimd.indirect_dma_start(
                        out=out, out_offset=bass.IndirectOffsetOnAxis(ap=sidx[h][:, 0:1], axis=0),
                        in_=y[n][h * CAP:(h + 1) * CAP, :], in_offset=None, compute_op=ALU.add).then_inc(added, 16)
                pool.wait_ge(added, 32 * k + 32)
                alone(pool)

            fetch(0, 0)
            fetch(1, 1)
            with nc.gpsimd.Fori(0, PAIRS // 2 - 1) as i:
                for n in range(2):
                    add(i, n)
                    fetch(2 * i + n + 2, n)
            for n in range(2):
                add(PAIRS // 2 - 1, n)

        @block.scalar
        def _(act):
            with nc.scalar.Fori(0, PAIRS // 2) as i:
                for n in range(2):
                    k = 2 * i + n
                    act.wait_ge(gx_turned, k + 1)
                    nc.scalar.copy(gxT[n][:, :, :], turn_ps[n].rearrange("p (c s) -> p c s", c=KC)).then_inc(gxT_in, 1)
                    act.wait_ge(hidden, k + 1)
                    nc.scalar.activation(eh[:, :], hidden_ps[n][:, 0:FF], ACT.Exp, scale=-1.0).then_inc(eh_in, 1)
                    act.wait_ge(g_turned, k + 1)
                    nc.scalar.copy(gT[n][:, 0, :], gate_ps[n][:, 0:P])
                    nc.scalar.copy(gT[n][0:FF - P, 1, :], gate_ps[n][0:FF - P, P:2 * P]).then_inc(gT_in, 1)

        @block.vector
        def _(dve):
            vec = nc.vector

            rounds = CAP // 8

            def earliest(src, dst, call):
                for r in range(rounds):
                    vec.max(dst[:, 8 * r:8 * r + 8], src).then_inc(pick, 1)
                    dve.wait_ge(pick, call * rounds + r + 1)
                    if r < rounds - 1:
                        vec.match_replace(src, dst[:, 8 * r:8 * r + 8], src, 0.0).then_inc(picked_out, 1)
                        dve.wait_ge(picked_out, call * (rounds - 1) + r + 1)

            earliest(keys[:, :], firsts[:, :], 0)
            dve.wait_ge(joined, 32)
            earliest(both[:, :], slot[:, :], 1)
            done = [0]

            def then(ins):
                done[0] += 1
                ins.then_inc(rows_in, 1)
                dve.wait_ge(rows_in, done[0])

            then(vec.tensor_scalar(sloti[:, :], slot[:, :], -1.0, float(TOKENS), ALU.mult, ALU.add))
            then(vec.tensor_scalar(low[:, :], sloti[:, :], B - 1, 8, ALU.bitwise_and, ALU.logical_shift_left))
            then(vec.tensor_scalar(high[:, :], sloti[:, :], 4, T - 1, ALU.logical_shift_right, ALU.bitwise_and))
            then(vec.tensor_tensor(tmp[:, :], low[:, :], high[:, :], ALU.add))
            then(vec.tensor_scalar(held[:, :], slot[:, :], 0.5, None, ALU.is_gt))
            then(vec.tensor_tensor(rowf[:, 0, :], tmp[:, :], held[:, :], ALU.mult))
            then(vec.tensor_copy(rowf[:, 1, :], rowf[:, 0, :]))
            then(vec.tensor_tensor(tmp[:, :], tab[0:EXPERTS, SPARE:SPARE + CAP], held[:, :], ALU.mult))
            then(vec.tensor_tensor(tmp[:, :], tab[0:EXPERTS, SPARE:SPARE + CAP], tmp[:, :], ALU.subtract))
            then(vec.tensor_tensor(rows_to[:, :], tmp[:, :], rowf[:, 0, :], ALU.add))
            dve.wait_ge(index_in, 1)
            dup = turn_ps[0][:, 0:EXPERTS].rearrange("p (k e) -> p k e", e=2)
            vec.tensor_copy(from_idx[0:CAP, :], dup[0:CAP, :, 0])
            vec.tensor_copy(from_idx[CAP:P, :], dup[CAP:P, :, 1])
            vec.tensor_copy(to_idx[:, :], turn_ps[1][0:CAP, 0:EXPERTS]).then_inc(index_in, 1)
            with nc.vector.Fori(0, PAIRS // 2) as i:
                for m in range(2):
                    k = 2 * i + m
                    dve.wait_ge(gx_in[m], i * 16 + 16)
                    alone(dve)
                    vec.tensor_copy(wcol[m][0:CAP, :], gx[m][0:CAP, bass.ds(D + 2 * k, 1)])
                    vec.tensor_copy(wcol[m][CAP:P, :], gx[m][CAP:P, bass.ds(D + 1 + 2 * k, 1)]).then_inc(wcol_in, 1)
                    dve.wait_ge(eh_in, k + 1)
                    alone(dve)
                    vec.tensor_scalar(sig[:, :], eh[:, :], 1.0, None, ALU.add).then_inc(moe_step, 1)
                    dve.wait_ge(moe_step, 3 * k + 1)
                    vec.reciprocal(gate[:, :], sig[:, :]).then_inc(moe_step, 1)
                    dve.wait_ge(moe_step, 3 * k + 2)
                    vec.tensor_tensor(sig[:, :], hidden_ps[m][:, 0:FF], gate[:, :], ALU.mult).then_inc(moe_step, 1)
                    dve.wait_ge(moe_step, 3 * k + 3)
                    vec.tensor_tensor(g[m][:, :], hidden_ps[m][:, FF:2 * FF], sig[:, :], ALU.mult).then_inc(g_in, 1)
                    dve.wait_ge(wcol_in, k + 1)
                    dve.wait_ge(y_full, k + 1)
                    vec.tensor_scalar(y[m][:, :], y_ps[m], wcol[m][:, 0:1], None, ALU.mult).then_inc(y_in, 1)

        @block.tensor
        def _(pe):
            mm = nc.tensor.matmul
            pe.wait_ge(rows_in, 10)
            nc.tensor.transpose(turn_ps[0][:, 0:EXPERTS], rowf[:, :, :].rearrange("e a s -> e (a s)"), ident[0:EXPERTS, 0:EXPERTS])
            nc.tensor.transpose(turn_ps[1][0:CAP, 0:EXPERTS], rows_to[:, :], ident[0:EXPERTS, 0:EXPERTS]).then_inc(index_in, 1)
            pe.wait_ge(index_in, 2)
            with nc.tensor.Fori(0, PAIRS // 2) as i:
                for n in range(2):
                    k = 2 * i + n
                    pe.wait_ge(gx_in[n], i * 16 + 16)
                    for c in range(KC):
                        ins = nc.tensor.transpose(turn_ps[n][:, c * P:(c + 1) * P], gx[n][:, c * P:(c + 1) * P], ident)
                    ins.then_inc(gx_turned, 1)
                    pe.wait_ge(gxT_in, k + 1)
                    for h in range(2):
                        pe.wait_ge(w_in[2 * n + h], i * 48 + 48)
                    alone(pe)
                    for c in range(KC):
                        for h in range(2):
                            ins = mm(hidden_ps[n][h * CAP:(h + 1) * CAP, :], gxT[n][:, c, h * CAP:(h + 1) * CAP],
                                     w13_sb[2 * n + h][:, c, :], start=(c == 0), stop=(c == KC - 1), skip_group_check=True)
                    ins.then_inc(hidden, 1)
                    pe.wait_ge(g_in, k + 1)
                    nc.tensor.transpose(gate_ps[n][:, 0:P], g[n][:, 0:P], ident)
                    nc.tensor.transpose(gate_ps[n][0:FF - P, P:2 * P], g[n][:, P:FF], ident).then_inc(g_turned, 1)
                    pe.wait_ge(gT_in, k + 1)
                    alone(pe)
                    for h in range(2):
                        s = slice(h * CAP, (h + 1) * CAP)
                        mm(y_ps[n][s, :], gT[n][:, 0, s], w2a_sb[2 * n + h][:, :], start=True, stop=False, skip_group_check=True)
                    for h in range(2):
                        s = slice(h * CAP, (h + 1) * CAP)
                        ins = mm(y_ps[n][s, :], gT[n][0:FF - P, 1, s], w2b_sb[2 * n + h][:, :], start=False, stop=True,
                                 skip_group_check=True)
                    ins.then_inc(y_full, 1)


def constants():
    tabs = np.zeros((P, TAB), np.float32)
    tabs[:, IDENT:IDENT + P] = np.eye(P)
    tri = np.where(np.arange(P)[None, :] > np.arange(P)[:, None], MASKED, 0.0)
    tabs[:, TRI:TRI + 4 * P] = np.tile(tri, (1, 4))
    tabs[:, HEADS:HEADS + P] = np.kron(np.eye(P // HD), np.full((HD, HD), 1.0 / HD))
    inv = (1.0 / np.float32(10000.0) ** (np.arange(0, DH, 2, dtype=np.float32) / np.float32(DH))).astype(np.float32)
    angle = (np.arange(T, dtype=np.float32)[:, None] * inv[None, :]).astype(np.float32).astype(np.float64)
    for t in range(TT):
        a = angle[t * P:(t + 1) * P]
        tabs[:, COS + t * DH:COS + (t + 1) * DH] = np.concatenate([np.cos(a), np.cos(a)], 1)
        tabs[:, SIN + t * DH:SIN + (t + 1) * DH] = np.concatenate([-np.sin(a), np.sin(a)], 1)
        tabs[:, KEY0 + t] = TOKENS - B * (t * P + np.arange(P))
    tabs[:, SPARE:SPARE + CAP] = TOKENS + np.arange(CAP)
    return tabs


def chunks(w):
    return np.ascontiguousarray(w.reshape(-1, P, w.shape[-1]).transpose(1, 0, 2))


def kernel(x, ctx_2048, L0_attn_Wq, L0_attn_Wk, L0_attn_Wv, L0_attn_Wo, L0_attn_lambda_q1, L0_attn_lambda_k1,
           L0_attn_lambda_q2, L0_attn_lambda_k2, L0_attn_gn_w, L0_attn_gn_b, L0_xattn_QW, L0_xattn_Qb, L0_xattn_KW,
           L0_xattn_Kb, L0_xattn_VW, L0_xattn_Vb, L0_ffn_router_w, L0_ffn_w1, L0_ffn_v1, L0_ffn_w2):
    import concourse.bacc as bacc
    from concourse.bass_utils import run_bass_kernel_spmd

    heads = np.array([[4 * (2 * (j // 4) + h) + j % 4 for h in range(2)] for j in range(UNITS)]).reshape(-1)
    pairs = np.concatenate([np.arange(0, DH, 2), np.arange(1, DH, 2)])
    inner = np.concatenate([i * DH + pairs for i in range(2)])
    q_cols = (heads[:, None] * HD + inner[None, :]).reshape(-1)
    k_cols = (np.arange(KV)[:, None] * HD + inner[None, :]).reshape(-1)
    o_rows = (heads[:, None] * HD + np.arange(HD)[None, :]).reshape(-1)
    a = {k: np.asarray(w) for k, w in locals().items() if k.startswith("L0_")}

    def columns(v):
        return v.reshape(-1, P).T

    lams = np.concatenate([a[f"L0_attn_lambda_{n}"] for n in ("q1", "k1", "q2", "k2")])
    cols = np.concatenate([columns(a["L0_attn_gn_w"][o_rows]), columns(a["L0_attn_gn_b"][o_rows]),
                           columns(a["L0_xattn_Qb"]), columns(a["L0_xattn_Kb"]), columns(a["L0_xattn_Vb"]),
                           np.broadcast_to(lams, (P, 4 * DH))], axis=1)
    w13 = np.concatenate([a["L0_ffn_w1"], a["L0_ffn_v1"]], axis=1)
    w13 = w13.transpose(0, 2, 1).reshape(EXPERTS, KC, P, 2 * FF).transpose(0, 2, 1, 3)
    arrays = {
        "x": np.asarray(x).reshape(TOKENS, D),
        "ctx": np.asarray(ctx_2048).reshape(TOKENS, D),
        "wqkv": chunks(np.concatenate([a["L0_attn_Wq"][:, q_cols], a["L0_attn_Wk"][:, k_cols], a["L0_attn_Wv"]], 1)),
        "wo": chunks(a["L0_attn_Wo"][o_rows]),
        "wx": np.stack([chunks(a[f"L0_xattn_{n}W"].T) for n in "QKV"], 1),
        "wr": chunks(a["L0_ffn_router_w"].T),
        "cols": cols,
        "tabs": constants(),
        "w13": w13.reshape(EXPERTS * P, KC * 2 * FF),
        "w2": a["L0_ffn_w2"].reshape(EXPERTS * FF, D),
    }
    arrays = {k: np.ascontiguousarray(v) for k, v in arrays.items()}
    nc = bacc.Bacc("TRN2", target_bir_lowering=False, num_devices=1)
    args = [nc.dram_tensor(k, v.shape, FP32, kind="ExternalInput").ap() for k, v in arrays.items()]
    out = nc.dram_tensor("out", (TOKENS + CAP, D), FP32, kind="ExternalOutput").ap()
    table = nc.dram_tensor("table", (TOKENS, ROW), FP32, kind="Internal").ap()
    build(nc, *args, out, table)
    r = run_bass_kernel_spmd(nc, [arrays], core_ids=[0])
    return r.results[0]["out"][:TOKENS].reshape(B, T, D)
```

```python
import math
from contextlib import ExitStack

import numpy as np

import concourse.bass as bass
from concourse import mybir

FP32 = mybir.dt.float32
BF16 = mybir.dt.bfloat16
I32 = mybir.dt.int32
ALU = mybir.AluOpType
ACT = mybir.ActivationFunctionType
AX = mybir.AxisListType

P = 128
B, T, D = 16, 256, 512
H, KV, DH = 16, 4, 32
TT = T // P
KC = D // P
HD = 2 * DH
UNITS = H // 2
NQK = 2 * H * DH + 2 * KV * DH
NQKV = NQK + KV * HD
ROPE_PARTS = [(0, 512), (512, 512), (1024, 256)]
BANK = 512
EXPERTS, TOPK, FF, CAP = 64, 8, 192, 64
TOKENS = B * T
ROW = D + EXPERTS
PAIRS = EXPERTS // 2
LAMBDA_INIT = 0.8 - 0.6 * math.exp(0.0)
EPS = 1e-5
SCALE = 1.0 / math.sqrt(DH)
MASKED = -1e30
LATE = B - 2
STEPS = [0, 2, 30, 9, 9]

IDENT, TRI, HEADS, COS, SIN, KEY0, SPARE, TAB = 0, 128, 640, 768, 832, 896, 898, 962
GW, GB, QB, KB, VB, LAM, COLS = 0, 8, 16, 18, 20, 22, 150


class Ring:

    def __init__(self, banks, names, before, lead, per, r):
        self.names, self.done, self.at = names, 0, {}
        before = dict(before)
        for n, name in enumerate(names):
            bank = banks[(lead + n) % len(banks)]
            before[bank] = before.get(bank, 0) + 1
            self.at[name] = (bank, before[bank])
        self.per, self.r = per, r

    def __getitem__(self, name):
        bank, turn = self.at[name]
        return bank, (turn if self.r is None else self.r * self.per + (turn - 2 * self.per))

    def next(self, name):
        assert self.names[self.done] == name, (self.names[self.done], name)
        self.done += 1
        return self[name]

    def ended(self):
        assert self.done == len(self.names)


def turn_names(stages):
    s1, s2, s3, s4 = (n in stages for n in (1, 2, 3, 4))
    score, turns, sums = [], [], []
    for s in range(UNITS + 3):
        if s2:
            score += [f"s{s}{part}" for part in "ABC"] * (s < UNITS)
            turns += [f"dT{s - 1}{h}" for h in range(2)] * (1 <= s <= UNITS)
            sums += [f"oT{s - 3}"] * (s >= 3) + [f"pv{s - 2}"] * (2 <= s < UNITS + 2)
        score += [f"x{q}" for q in range(4)] * (s3 and s == 5)
        turns += {2: ["xnT0", "xnT1"] * s1, 3: ["rT0", "rT1"] * s4, 7: ["pT0", "pT1", "pT2", "pT3"] * s3,
                  8: ["keyT"] * s4 + ["kT", "qT0", "qT1"] * s1, 10: ["qT2", "qT3"] * s1}.get(s, [])
        sums += {0: ["kx1", "wo0"] * s3, 1: ["wo1"] * s3, 2: ["vx0"] * s3, 3: ["qa0", "qb0"] * s1,
                 4: ["qx0", "qx1"] * s3 + ["route0", "route1"] * s4, 5: ["kv0", "qa1"] * s1, 6: ["vx1"] * s3,
                 7: ["qb1"] * s1, 8: ["kv1"] * s1 + ["h0", "h1"] * s3, 10: ["gmean", "kx0", "gvar"] * s2}.get(s, [])
    return score, turns, sums


class Round:

    BANKS = ([0, 1, 2, 3], [4, 5], [6, 7])

    def __init__(self, key, stages, used):
        self.key, self.stages, self.names = key, stages, turn_names(stages)
        self.before = [dict(u) for u in used[0]]
        self.lead = list(used[1])
        repeats = B - 3 if key == "loop" else 1
        for k, names in enumerate(self.names):
            banks = self.BANKS[k]
            assert key != "loop" or len(names) % len(banks) == 0
            for n in range(len(names)):
                bank = banks[(self.lead[k] + n) % len(banks)]
                used[0][k][bank] = used[0][k].get(bank, 0) + repeats
            used[1][k] = (self.lead[k] + repeats * len(names)) % len(banks)

    def at(self, r):
        r = r if self.key == "loop" else None
        return [Ring(self.BANKS[k], names, self.before[k], self.lead[k], len(names) // len(self.BANKS[k]), r)
                for k, names in enumerate(self.names)]

    def first(self, stage):
        return self.key == stage - 2


def all_rounds():
    used = ([{}, {}, {}], [0, 0, 0])
    stages = {-1: (1,), 0: (1, 2), 1: (1, 2, 3), "loop": (1, 2, 3, 4), B - 1: (2, 3, 4), B: (3, 4), B + 1: (4,)}
    return {key: Round(key, s, used) for key, s in stages.items()}


ROUNDS = all_rounds()

def build(nc, x, ctx, wqkv, wo, wx, wr, cols, tabs, w13, w2, out, table):
    with ExitStack() as stack:
        psum = stack.enter_context(nc.psum_tensor("psum", [P, 8, BANK], FP32))
        keys = stack.enter_context(nc.sbuf_tensor("keys", [P, B * P], FP32))
        tab = stack.enter_context(nc.sbuf_tensor("tab", [P, TAB], FP32))
        with ExitStack() as st:
            attention(nc, st, psum, x, ctx, wqkv, wo, wx, wr, cols, tabs, out, table, keys, tab)
        with ExitStack() as st:
            experts(nc, st, psum, w13, w2, out, table, keys, tab)


def alone(eng):
    eng.nop(nofuse=True)


def attention(nc, st, psum, x, ctx, wqkv, wo, wx, wr, cols, tabs, out, table, keys, tab):
    def sb(name, shape, dt=FP32):
        return st.enter_context(nc.sbuf_tensor(name, shape, dt))

    def sem(name):
        return st.enter_context(nc.semaphore(name))

    wqkv_sb = sb("wqkv_sb", [P, KC, NQKV])
    wo_sb = sb("wo_sb", [P, UNITS, D])
    wx_sb = sb("wx_sb", [P, 3, TT, T])
    wr_sb = sb("wr_sb", [P, KC, EXPERTS])
    col = sb("col", [P, COLS])
    ident = tab[:, IDENT:IDENT + P]
    ident_b = sb("ident_b", [P, P], BF16)
    tri_b = sb("tri_b", [P, 4, P], BF16)
    gnw, gnb = sb("gnw", [P, UNITS]), sb("gnb", [P, UNITS])
    half = sb("half", [P, UNITS])
    prod, dots, lam, neglam = sb("prod", [P, 2, DH]), sb("dots", [P, 2]), sb("lam", [P, 2]), sb("neglam", [P, 1])
    keycol = sb("keycol", [P, TT])

    xt, ct, xn, xn2 = (sb(n, [P, TT, D]) for n in ("xt", "ct", "xn", "xn2"))
    xnT = sb("xnT", [P, KC, T])
    rope1, rope2 = sb("rope1", [P, 2, BANK]), sb("rope2", [P, 2, BANK])
    qk = sb("qk", [P, TT, NQK])
    qT = sb("qT", [P, UNITS, T])
    kz = sb("kz", [P, 2, 4, T])
    v, v_next = sb("v", [P, TT, KV * HD]), sb("v_next", [P, TT, KV * HD])
    ex = sb("ex", [P, 2, 4, 3 * P])
    diff = sb("diff", [P, 2, 2, 3 * P])
    diffT = sb("diffT", [P, 2, 2, 3 * P])
    osc = sb("osc", [P, 2, TT, P])
    oT = sb("oT", [P, UNITS, T])
    x1 = sb("x1", [P, TT, D])
    qx, kx, vx = sb("qx", [P, 2, D]), sb("kx", [P, 2, D]), sb("vx", [P, 4, T])
    pr, prT = sb("pr", [P, 4, D]), sb("prT", [P, 4, D])
    row = sb("row", [P, TT, ROW])
    rT = sb("rT", [P, KC, T])
    st6, mv, ve, rstd = sb("st6", [P, 6, 6]), sb("mv", [P, 6, 2]), sb("ve", [P, 6]), sb("rstd", [P, 6])
    mx, nm, den, rden = (sb(n, [P, 2, 8]) for n in ("mx", "nm", "den", "rden"))
    cmul = sb("cmul", [P, 2, 4])
    go6, gmv = sb("go6", [P, UNITS, 6]), sb("gmv", [P, UNITS, 2])
    gm, gdev, gsq, gve, grs, ga, gb = (sb(n, [P, UNITS]) for n in ("gm", "gdev", "gsq", "gve", "grs", "ga", "gb"))
    mxx, nmx, denx, rdenx = (sb(n, [P, 4]) for n in ("mxx", "nmx", "denx", "rdenx"))
    rmx, rnm, rden1, rr, s8, r8 = (sb(n, [P, TT]) for n in ("rmx", "rnm", "rden1", "rr", "s8", "r8"))
    prob, rest, chosen, pexp, keyed = (sb(n, [P, TT, EXPERTS]) for n in ("prob", "rest", "chosen", "pexp", "keyed"))
    top = sb("top", [P, TT, TOPK])
    early = sb("early", [P, CAP])

    consts_in, later_in = sem("consts_in"), sem("later_in")
    wqkv_in = [sem(f"wqkv_in{n}") for n in range(3)]
    made = sem("made")
    zeroed = sem("zeroed")
    lam_exp = sem("lam_exp")
    x_in, ctx_in, x1_load = sem("x_in"), sem("ctx_in"), sem("x1_load")
    full = [sem(f"bank{n}_full") for n in range(8)]
    free = [sem(f"bank{n}_free") for n in range(8)]
    stats, ve_in, rooted, normed = ([sem(f"{n}_{m}") for m in ("first", "later")]
                                    for n in ("stats", "ve_in", "rooted", "normed"))
    k_roped, rope_sum = sem("k_roped"), sem("rope_sum")
    v_in = sem("v_in")
    max_in, diff_in = sem("max_in"), sem("diff_in")
    gstat, groot, gdone = sem("gstat"), sem("groot"), sem("gdone")
    xmax, xnorm = sem("xmax"), sem("xnorm")
    row_in, rmax_in = sem("row_in"), sem("rmax_in")
    early_step = sem("early_step")
    out_done, row_done = sem("out_done"), sem("row_done")
    step = [None] + [sem(f"step{n}") for n in range(1, 5)]

    def begin(eng, ring, name):
        bank, turn = ring.next(name)
        eng.wait_ge(free[bank], turn)
        return psum[:, bank, :], full[bank]

    def filled(eng, ring, name):
        bank, turn = ring[name]
        eng.wait_ge(full[bank], turn)
        return psum[:, bank, :], free[bank]

    def emptied(eng, ring, name):
        bank, turn = ring[name]
        eng.wait_ge(free[bank], turn + 1)

    def rounds(fori, body):
        for r in range(-1, 2):
            body(r, ROUNDS[r])
        with fori(2, B - 1) as r:
            body(r, ROUNDS["loop"])
        for r in range(B - 1, B + 2):
            body(r, ROUNDS[r])

    block_context = nc.Block()
    block = block_context.__enter__()

    @block.sync
    def _(sp):
        def rows_of(a, i):
            return a[bass.ds(i * T, T), :].rearrange("(t p) d -> p t d", p=P)

        sp.dma_start(tab[:, :], tabs).then_inc(consts_in, 16)
        sp.dma_start(xt[:, :, :], rows_of(x, 0)).then_inc(x_in, 16)
        sp.dma_start(col[:, :], cols).then_inc(consts_in, 16)
        for n in range(3):
            s = slice(n * BANK, (n + 1) * BANK)
            sp.dma_start(wqkv_sb[:, :, s], wqkv[:, :, s]).then_inc(wqkv_in[n], 16)
        for dst, src in ((wo_sb[:, :, :], wo), (wx_sb[:, :, :, :], wx), (wr_sb[:, :, :], wr)):
            sp.dma_start(dst, src).then_inc(later_in, 16)
        sp.dma_start(ct[:, :, :], rows_of(ctx, 0)).then_inc(ctx_in, 16)

        def body(r, rd, more=True):
            score, turns, sums = rd.at(r)
            if 3 in rd.stages:
                b = r - 1
                if not rd.first(3):
                    sp.wait_ge(out_done, 16 * b)
                    alone(sp)
                    sp.wait_ge(normed[1], 2 * TT * b)
                    alone(sp)
                sp.dma_start(x1[:, :, :], rows_of(x, b)).then_inc(x1_load, 16)
            if 1 in rd.stages and more:
                sp.wait_ge(normed[0], TT * (r + 2))
                alone(sp)
                sp.dma_start(xt[:, :, :], rows_of(x, r + 2)).then_inc(x_in, 16)
            if 3 in rd.stages and 2 in rd.stages:
                bank, turn = sums["vx1"]
                sp.wait_ge(full[bank], turn)
                alone(sp)
                sp.dma_start(ct[:, :, :], rows_of(ctx, r)).then_inc(ctx_in, 16)
            if 4 in rd.stages:
                sp.wait_ge(row_in, r - 1)
                alone(sp)
                sp.dma_start(rows_of(table, r - 2), row[:, :, :]).then_inc(row_done, 16)
            if 3 in rd.stages:
                emptied(sp, sums, "h1")
                alone(sp)
                sp.dma_start(rows_of(out, r - 1), x1[:, :, :]).then_inc(out_done, 16)

        for r in range(-1, 2):
            body(r, ROUNDS[r])
        with nc.sync.Fori(2, B - 2) as r:
            body(r, ROUNDS["loop"])
        body(B - 2, ROUNDS["loop"], more=False)
        for r in range(B - 1, B + 2):
            body(r, ROUNDS[r])
        sp.wait_ge(out_done, 16 * B)
        sp.wait_ge(row_done, 16 * B)

    @block.gpsimd
    def _(pool):
        nc.gpsimd.memset(half[:, :], -0.5).then_inc(zeroed, 1)
        nc.gpsimd.memset(kz[:, :, :, :], 0.0).then_inc(zeroed, 1)
        pool.wait_ge(zeroed, 2)

        def body(r, rd):
            score, turns, sums = rd.at(r)
            s1, s2, s3 = (n in rd.stages for n in (1, 2, 3))

            def root(later, b, n):
                k, per = 2 * later + n, (2 * TT if later else TT)
                pool.wait_ge(stats[later], b * per + (n + 1))
                alone(pool)
                nc.gpsimd.tensor_scalar(ve[:, k:k + 1], mv[:, k, 1:2], EPS, None, ALU.add).then_inc(ve_in[later], 1)
                pool.wait_ge(ve_in[later], b * per + (n + 1))
                nc.gpsimd.tensor_tensor(rstd[:, k:k + 1], ve[:, k:k + 1], half[:, 0:1], ALU.pow).then_inc(rooted[later], 1)

            def rope(k):
                lo, n = ROPE_PARTS[k % 3]
                if k % 3 < 2:
                    emptied(pool, sums, ("qa", "qb")[k % 3] + str(k // 3))
                else:
                    pool.wait_ge(k_roped, (r + 1) * TT + (k // 3 + 1))
                nc.gpsimd.tensor_tensor(qk[:, k // 3, lo:lo + n], rope1[:, k % 2, 0:n], rope2[:, k % 2, 0:n],
                                        ALU.add).then_inc(rope_sum, 1)

            if s1:
                root(0, r + 1, 0)
                root(0, r + 1, 1)
            if s3:
                root(1, r - 1, 0)
                root(1, r - 1, 1)
            if s1:
                for k in range(6):
                    rope(k)
            if s3:
                root(1, r - 1, 2)
                root(1, r - 1, 3)
            if s2:
                emptied(pool, sums, "gvar")
                nc.gpsimd.tensor_tensor(grs[:, :], gve[:, :], half[:, :], ALU.pow).then_inc(groot, 1)
            if s1:
                emptied(pool, sums, "kv0")
                emptied(pool, sums, "kv1")
                if s2:
                    filled(pool, sums, f"pv{UNITS - 1}")
                alone(pool)
                nc.gpsimd.tensor_copy(v[:, :, :], v_next[:, :, :]).then_inc(v_in, 1)

        rounds(nc.gpsimd.Fori, body)

    @block.scalar
    def _(act):
        act.wait_ge(zeroed, 2)
        act.wait_ge(made, 3)
        nc.scalar.activation(lam[:, :], dots[:, :], ACT.Exp).then_inc(lam_exp, 1)

        def body(r, rd):
            score, turns, sums = rd.at(r)
            s1, s2, s3, s4 = (n in rd.stages for n in (1, 2, 3, 4))

            def exponentials(j):
                act.wait_ge(max_in, r * UNITS + (j + 1))
                for t in range(TT):
                    for q in range(4):
                        bank, _ = score[f"s{j}" + ("A" if t == 0 else "BC"[q // 2])]
                        lo, n = (q * P, P) if t == 0 else (q % 2 * T, T)
                        k = 4 * t + q
                        ins = nc.scalar.activation(ex[:, j % 2, q, t * P:t * P + n], psum[:, bank, lo:lo + n], ACT.Exp,
                                                   bias=nm[:, j % 2, k:k + 1], scale=SCALE,
                                                   accum_out=den[:, j % 2, k:k + 1])
                        if q == 3 or (t == 1 and q == 1):
                            ins.then_inc(free[bank], 1)

            def turned(j):
                for h in range(2):
                    ps, freed = filled(act, turns, f"dT{j}{h}")
                    nc.scalar.copy(diffT[:, j % 2, h, :], ps[:, 0:3 * P]).then_inc(freed, 1)

            def unit(s):
                if s2 and 1 <= s <= UNITS:
                    turned(s - 1)
                if s2 and s < UNITS:
                    exponentials(s)

            def value(t):
                ps, freed = filled(act, sums, f"kv{t}")
                act.wait_ge(k_roped, (r + 1) * TT + (t + 1))
                nc.scalar.copy(v_next[:, t, :], ps[:, 256:512]).then_inc(freed, 1)

            def halves(ring, name, dst):
                ps, freed = filled(act, ring, name)
                nc.scalar.copy(dst, ps.rearrange("p (a b) -> p a b", a=dst.shape[1])).then_inc(freed, 1)

            def biased(name, n, bias):
                ps, freed = filled(act, sums, name)
                dst = kx if name[0] == "k" else qx
                nc.scalar.activation(dst[:, n, :], ps, ACT.Identity, bias=col[:, bias + n:bias + n + 1]).then_inc(freed, 1)

            unit(0)
            if s3:
                biased("kx1", 1, KB)
            unit(1)
            unit(2)
            if s3:
                halves(sums, "vx0", vx[:, 0:2, :])
            unit(3)
            unit(4)
            if s3:
                biased("qx0", 0, QB)
                biased("qx1", 1, QB)
            if s4:
                for t in range(TT):
                    act.wait_ge(rmax_in, (r - 2) * TT + (t + 1))
                    bank, _ = sums[f"route{t}"]
                    nc.scalar.activation(pexp[:, t, :], psum[:, bank, 0:EXPERTS], ACT.Exp, bias=rnm[:, t:t + 1],
                                         scale=1.0, accum_out=rden1[:, t:t + 1]).then_inc(free[bank], 1)
            unit(5)
            if s3:
                for q in range(4):
                    act.wait_ge(xmax, (r - 1) * 4 + (q + 1))
                    bank, _ = score[f"x{q}"]
                    nc.scalar.activation(pr[:, q, :], psum[:, bank, :], ACT.Exp, bias=nmx[:, q:q + 1], scale=1.0,
                                         accum_out=denx[:, q:q + 1]).then_inc(free[bank], 1)
            if s1:
                value(0)
            unit(6)
            if s3:
                halves(sums, "vx1", vx[:, 2:4, :])
            unit(7)
            if s3:
                for q in range(4):
                    halves(turns, f"pT{q}", prT[:, :, q * P:(q + 1) * P])
            unit(8)
            if s1:
                value(1)
                ps, freed = filled(act, turns, "kT")
                for q in range(4):
                    rows = slice(DH * q, DH * q + DH)
                    ins = nc.scalar.copy(kz[rows, :, q, :], ps[rows, :].rearrange("p (a b) -> p a b", a=2))
                ins.then_inc(freed, 1)
                for n in range(4):
                    halves(turns, f"qT{n}", qT[:, 2 * n:2 * n + 2, :])
            if s2:
                biased("kx0", 0, KB)

        rounds(nc.scalar.Fori, body)

    @block.vector
    def _(dve):
        vec = nc.vector
        dve.wait_ge(consts_in, 16 * 2)
        vec.tensor_tensor(prod[:, 0, :], col[:, LAM:LAM + DH], col[:, LAM + DH:LAM + 2 * DH], ALU.mult)
        vec.tensor_tensor(prod[:, 1, :], col[:, LAM + 2 * DH:LAM + 3 * DH], col[:, LAM + 3 * DH:LAM + 4 * DH],
                          ALU.mult).then_inc(made, 1)
        vec.tensor_scalar(gnw[:, :], col[:, GW:GW + UNITS], 1.0 - LAMBDA_INIT, None, ALU.mult)
        vec.tensor_scalar(gnb[:, :], col[:, GB:GB + UNITS], 1.0 - LAMBDA_INIT, None, ALU.mult)
        vec.tensor_copy(ident_b[:, :], ident)
        vec.tensor_copy(tri_b[:, :, :], tab[:, TRI:TRI + 4 * P].rearrange("p (a b) -> p a b", a=4)).then_inc(made, 1)
        dve.wait_ge(made, 2)
        vec.tensor_reduce(dots[:, :], prod[:, :, :], AX.X, ALU.add).then_inc(made, 1)
        vec.tensor_copy(keycol[:, :], tab[:, KEY0:KEY0 + TT]).then_inc(made, 1)
        dve.wait_ge(lam_exp, 1)
        vec.scalar_tensor_tensor(out=neglam[:, :], in0=lam[:, 1:2], scalar=LAMBDA_INIT, in1=lam[:, 0:1],
                                 op0=ALU.subtract, op1=ALU.subtract).then_inc(made, 1)
        dve.wait_ge(made, 5)
        dve.wait_ge(zeroed, 2)

        def body(r, rd):
            score, turns, sums = rd.at(r)
            s1, s2, s3, s4 = (n in rd.stages for n in (1, 2, 3, 4))
            batch = [None, r + 1, r, r - 1, r - 2]
            steps = [0] * 5

            def after(stage, ins):
                steps[stage] += 1
                ins.then_inc(step[stage], 1)
                dve.wait_ge(step[stage], batch[stage] * STEPS[stage] + steps[stage])

            def measure(later, n, src):
                k = 2 * later + n
                after(3 if later else 1, vec.bn_stats(st6[:, k, :], src))
                alone(dve)
                vec.bn_aggr(mv[:, k, :], st6[:, k, :]).then_inc(stats[later], 1)

            def normalise(later, n, src, dst):
                k, per = 2 * later + n, (2 * TT if later else TT)
                dve.wait_ge(rooted[later], batch[3 if later else 1] * per + (n + 1))
                vec.tensor_scalar(dst, src, mv[:, k, 0:1], rstd[:, k:k + 1], ALU.subtract, ALU.mult).then_inc(normed[later], 1)

            def halves(ring, name, dst):
                ps, freed = filled(dve, ring, name)
                vec.tensor_copy(dst, ps.rearrange("p (a b) -> p a b", a=dst.shape[1])).then_inc(freed, 1)

            def rope(k):
                t, part = divmod(k, 3)
                ps, freed = filled(dve, sums, ("qa", "qb", "kv")[part] + str(t))
                if k >= 2:
                    dve.wait_ge(rope_sum, (r + 1) * (3 * TT) + (k - 1))
                n = ROPE_PARTS[part][1]
                g, h = n // DH, DH // 2
                src = ps[:, 0:n].rearrange("p (g d) -> p g d", d=DH)
                a = rope1[:, k % 2, 0:n].rearrange("p (g d) -> p g d", d=DH)
                b = rope2[:, k % 2, 0:n].rearrange("p (g d) -> p g d", d=DH)
                cos = tab[:, COS + t * DH:COS + (t + 1) * DH]
                sin = tab[:, SIN + t * DH:SIN + (t + 1) * DH]
                vec.tensor_tensor(b[:, :, 0:h], src[:, :, h:DH], sin[:, 0:h].unsqueeze(1).broadcast_to([P, g, h]), ALU.mult)
                vec.tensor_tensor(b[:, :, h:DH], src[:, :, 0:h], sin[:, h:DH].unsqueeze(1).broadcast_to([P, g, h]), ALU.mult)
                ins = vec.tensor_tensor(a, src, cos.unsqueeze(1).broadcast_to([P, g, DH]), ALU.mult)
                ins.then_inc(freed if part < 2 else k_roped, 1)

            def maxima(j):
                for part, at in zip("ABC", (0, 4, 6)):
                    ps, _ = filled(dve, score, f"s{j}{part}")
                    n = 4 if part == "A" else 2
                    ins = vec.tensor_reduce(mx[:, j % 2, at:at + n], ps.rearrange("p (a b) -> p a b", a=n), AX.X, ALU.max)
                after(2, ins)
                vec.tensor_scalar(nm[:, j % 2, :], mx[:, j % 2, :], -SCALE, None, ALU.mult).then_inc(max_in, 1)

            def difference(j):
                if j >= 2:
                    emptied(dve, sums, f"pv{j - 2}")
                emptied(dve, score, f"s{j}C")
                after(2, vec.reciprocal(rden[:, j % 2, :], den[:, j % 2, :]))
                d = den[:, j % 2, :].rearrange("p (a i) -> p a i", i=2)
                rd_ = rden[:, j % 2, :].rearrange("p (a i) -> p a i", i=2)
                after(2, vec.scalar_tensor_tensor(out=cmul[:, j % 2, :], in0=rd_[:, :, 1], scalar=neglam[:, 0:1],
                                                  in1=d[:, :, 0], op0=ALU.mult, op1=ALU.mult))
                for t in range(TT):
                    for h in range(2):
                        s = slice(t * P, P + 2 * t * P)
                        ins = vec.scalar_tensor_tensor(out=diff[:, j % 2, h, s], in0=ex[:, j % 2, 2 * h + 1, s],
                                                       scalar=cmul[:, j % 2, 2 * t + h:2 * t + h + 1],
                                                       in1=ex[:, j % 2, 2 * h, s], op0=ALU.mult, op1=ALU.add)
                ins.then_inc(diff_in, 1)

            def scaled(j):
                ps, freed = filled(dve, sums, f"pv{j}")
                r1 = rden[:, j % 2, :].rearrange("p (a i) -> p a i", i=2)[:, :, 0:1].broadcast_to([P, 4, HD])
                vec.tensor_tensor(osc[:, j % 2, :, :].rearrange("p t (h d) -> p (t h) d", h=2),
                                  ps[:, 0:T].rearrange("p (a d) -> p a d", d=HD), r1, ALU.mult).then_inc(freed, 1)

            def collected(j):
                ps, freed = filled(dve, sums, f"oT{j}")
                vec.bn_stats(go6[:, j, :], ps[:, 0:T])
                vec.tensor_copy(oT[:, j, :], ps[:, 0:T]).then_inc(freed, 1)

            def unit(s, other=None):
                if s2 and 1 <= s <= UNITS:
                    difference(s - 1)
                if other:
                    other()
                if not s2:
                    return
                if s < UNITS:
                    maxima(s)
                if 3 <= s:
                    collected(s - 3)
                if 2 <= s < UNITS + 2:
                    scaled(s - 2)

            def residual(t):
                if t == 0:
                    dve.wait_ge(x1_load, r * 16)
                ps, freed = filled(dve, sums, f"wo{t}")
                vec.tensor_tensor(x1[:, t, :], x1[:, t, :], ps, ALU.add).then_inc(freed, 1)
                emptied(dve, sums, f"wo{t}")
                measure(1, t, x1[:, t, :])

            def earlier(n):
                src, dst = keys[:, 0:LATE * P], early[:, 8 * n:8 * n + 8]
                if n:
                    dve.wait_ge(early_step, 2 * n)
                alone(dve)
                vec.max(dst, src).then_inc(early_step, 1)
                dve.wait_ge(early_step, 2 * n + 1)
                alone(dve)
                vec.match_replace(src, dst, src, 0.0).then_inc(early_step, 1)

            def choose():
                emptied(dve, sums, "route0")
                emptied(dve, sums, "route1")
                after(4, vec.reciprocal(rr[:, :], rden1[:, :]))
                vec.tensor_scalar(prob[:, 0, :], pexp[:, 0, :], rr[:, 0:1], None, ALU.mult)
                after(4, vec.tensor_scalar(prob[:, 1, :], pexp[:, 1, :], rr[:, 1:2], None, ALU.mult))
                alone(dve)
                vec.max(top[:, 0, :], prob[:, 0, :])
                after(4, vec.max(top[:, 1, :], prob[:, 1, :]))
                after(4, vec.tensor_reduce(s8[:, :], top[:, :, :], AX.X, ALU.add))
                vec.reciprocal(r8[:, :], s8[:, :])
                vec.match_replace(rest[:, 0, :], top[:, 0, :], prob[:, 0, :], -1.0)
                after(4, vec.match_replace(rest[:, 1, :], top[:, 1, :], prob[:, 1, :], -1.0))
                after(4, vec.tensor_scalar(chosen[:, :, :], rest[:, :, :], 0.0, None, ALU.is_lt))
                for t in range(TT):
                    vec.tensor_scalar(keyed[:, t, :], chosen[:, t, :], keycol[:, t:t + 1], None, ALU.mult)
                    ins = vec.scalar_tensor_tensor(out=row[:, t, D:ROW], in0=prob[:, t, :], scalar=r8[:, t:t + 1],
                                                   in1=chosen[:, t, :], op0=ALU.mult, op1=ALU.mult)
                ins.then_inc(row_in, 1)

            if s1:
                dve.wait_ge(x_in, (r + 1) * 16 + 16)
                for t in range(TT):
                    measure(0, t, xt[:, t, :])
            unit(0)

            def gap0():
                if s1:
                    for t in range(TT):
                        normalise(0, t, xt[:, t, :], xn[:, t, :])
                if s3:
                    residual(0)

            def gap1():
                if s3:
                    residual(1)
                    normalise(1, 0, x1[:, 0, :], xn2[:, 0, :])

            def gap2():
                if s1:
                    halves(turns, "xnT0", xnT[:, 0:2, :])
                    halves(turns, "xnT1", xnT[:, 2:4, :])
                if s3:
                    normalise(1, 1, x1[:, 1, :], xn2[:, 1, :])

            def gap3():
                if s1:
                    rope(0)
                if s4:
                    halves(turns, "rT0", rT[:, 0:2, :])
                    halves(turns, "rT1", rT[:, 2:4, :])
                if s1:
                    rope(1)

            def gap4():
                if s4:
                    for t in range(TT):
                        ps, _ = filled(dve, sums, f"route{t}")
                        after(4, vec.tensor_reduce(rmx[:, t:t + 1], ps[:, 0:EXPERTS], AX.X, ALU.max))
                        vec.tensor_scalar(rnm[:, t:t + 1], rmx[:, t:t + 1], -1.0, None, ALU.mult).then_inc(rmax_in, 1)

            def gap5():
                if s3:
                    for q in range(4):
                        ps, _ = filled(dve, score, f"x{q}")
                        after(3, vec.tensor_reduce(mxx[:, q:q + 1], ps, AX.X, ALU.max))
                        vec.tensor_scalar(nmx[:, q:q + 1], mxx[:, q:q + 1], -1.0, None, ALU.mult).then_inc(xmax, 1)
                if s1:
                    rope(2)
                    rope(3)

            def gap6():
                if s3:
                    for q in range(4):
                        emptied(dve, score, f"x{q}")
                    after(3, vec.reciprocal(rdenx[:, :], denx[:, :]))
                    for q in range(4):
                        vec.tensor_scalar(pr[:, q, :], pr[:, q, :], rdenx[:, q:q + 1], None, ALU.mult).then_inc(xnorm, 1)

            def gap7():
                if s1:
                    rope(4)

            def gap8():
                if s1:
                    rope(5)
                if s4:
                    ps, freed = filled(dve, turns, "keyT")
                    after(4, vec.tensor_scalar(keycol[:, :], keycol[:, :], -1.0, None, ALU.add))
                    alone(dve)
                    vec.tensor_copy(keys[:, bass.ds((r - 2) * P, P)], ps[:, 0:P]).then_inc(freed, 1)
                if s3:
                    for t in range(TT):
                        ps, freed = filled(dve, sums, f"h{t}")
                        vec.scalar_tensor_tensor(out=x1[:, t, :], in0=ps, scalar=col[:, VB + t:VB + t + 1],
                                                 in1=x1[:, t, :], op0=ALU.add, op1=ALU.add).then_inc(freed, 1)
                        emptied(dve, sums, f"h{t}")
                        measure(1, TT + t, x1[:, t, :])

            def gap9():
                if s2:
                    emptied(dve, sums, f"oT{UNITS - 2}")
                    alone(dve)
                    for j in range(UNITS - 1):
                        vec.bn_aggr(gmv[:, j, :], go6[:, j, :])

            for s, other in enumerate((gap0, gap1, gap2, gap3, gap4, gap5, gap6, gap7, gap8, gap9)):
                unit(s + 1, other)
                if s4 and s == 6:
                    choose()
                if rd.key == B and s < CAP // 8:
                    earlier(s)
            if s2:
                emptied(dve, sums, f"oT{UNITS - 1}")
                alone(dve)
                vec.bn_aggr(gmv[:, UNITS - 1, :], go6[:, UNITS - 1, :]).then_inc(gstat, 1)
            if s3:
                if not rd.first(3):
                    dve.wait_ge(row_done, (r - 1) * 16)
                for t in range(TT):
                    normalise(1, TT + t, x1[:, t, :], row[:, t, 0:D])
            if s2:
                ps, freed = filled(dve, sums, "gmean")
                after(2, vec.tensor_copy(gm[:, :], ps[:, 0:UNITS]))
                after(2, vec.tensor_tensor(gdev[:, :], gmv[:, :, 0], gm[:, :], ALU.subtract))
                after(2, vec.tensor_tensor(gsq[:, :], gdev[:, :], gdev[:, :], ALU.mult))
                vec.tensor_tensor(gdev[:, :], gsq[:, :], gmv[:, :, 1], ALU.add).then_inc(freed, 1)
                ps, freed = filled(dve, sums, "gvar")
                vec.tensor_scalar(gve[:, :], ps[:, 0:UNITS], EPS, None, ALU.add).then_inc(freed, 1)
                dve.wait_ge(groot, r + 1)
                after(2, vec.tensor_tensor(ga[:, :], grs[:, :], gnw[:, :], ALU.mult))
                after(2, vec.tensor_tensor(gsq[:, :], gm[:, :], ga[:, :], ALU.mult))
                after(2, vec.tensor_tensor(gb[:, :], gnb[:, :], gsq[:, :], ALU.subtract))
                for j in range(UNITS):
                    ins = vec.tensor_scalar(oT[:, j, :], oT[:, j, :], ga[:, j:j + 1], gb[:, j:j + 1], ALU.mult, ALU.add)
                ins.then_inc(gdone, 1)
            for n in rd.stages:
                assert steps[n] == STEPS[n], (n, steps)

        rounds(nc.vector.Fori, body)
        dve.wait_ge(early_step, 2 * (CAP // 8))
        vec.tensor_copy(keys[:, LATE * P - CAP:LATE * P], early[:, :]).then_inc(early_step, 1)
        dve.wait_ge(early_step, 2 * (CAP // 8) + 1)

    @block.tensor
    def _(pe):
        for n in range(8):
            pe.sem_inc(free[n], 1)
        pe.wait_ge(consts_in, 16 * 2)
        pe.wait_ge(made, 2)

        def mm(out_, lhsT, rhs, start, stop):
            return nc.tensor.matmul(out_, lhsT, rhs, start=start, stop=stop)

        def body(r, rd):
            score, turns, sums = rd.at(r)
            s1, s2, s3, s4 = (n in rd.stages for n in (1, 2, 3, 4))

            def turn(name, pieces):
                ps, done = begin(pe, turns, name)
                for n, piece in enumerate(pieces):
                    ins = nc.tensor.transpose(ps[:, n * P:(n + 1) * P], piece, ident)
                ins.then_inc(done, 1)

            def product(name, groups, n=BANK):
                ps, done = begin(pe, sums, name)
                for g, pairs in enumerate(groups):
                    for k, (lhsT, rhs) in enumerate(pairs):
                        ins = mm(ps[:, g * n:(g + 1) * n], lhsT, rhs, k == 0, k == len(pairs) - 1)
                ins.then_inc(done, 1)

            def scores(j):
                g = j // 4
                ps, done = begin(pe, score, f"s{j}A")
                mm(ps, qT[:, j, 0:P], kz[:, g, :, 0:P], True, False)
                mm(ps, ident_b[:, :], tri_b[:, :, :], False, True).then_inc(done, 1)
                for k, part in enumerate("BC"):
                    ps, done = begin(pe, score, f"s{j}{part}")
                    mm(ps, qT[:, j, P:2 * P], kz[:, g, 2 * k:2 * k + 2, :], True, False)
                    mm(ps.rearrange("p (a b) -> p a b", a=2)[:, :, P:2 * P], ident_b[:, :], tri_b[:, 0:2, :],
                       False, True).then_inc(done, 1)

            def turn_difference(j):
                pe.wait_ge(diff_in, r * UNITS + (j + 1))
                for h in range(2):
                    turn(f"dT{j}{h}", [diff[:, j % 2, h, n * P:(n + 1) * P] for n in range(3)])

            def weigh(j):
                if j == 0:
                    pe.wait_ge(v_in, r + 1)
                emptied(pe, turns, f"dT{j}0")
                emptied(pe, turns, f"dT{j}1")
                ps, done = begin(pe, sums, f"pv{j}")
                for h in range(2):
                    vh = v[:, :, (2 * (j // 4) + h) * HD:(2 * (j // 4) + h + 1) * HD]
                    dT = diffT[:, j % 2, h, :]
                    mm(ps[:, h * HD:(h + 1) * HD], dT[:, 0:P], vh[:, 0, :], True, True)
                    mm(ps[:, P + h * HD:P + (h + 1) * HD], dT[:, P:2 * P], vh[:, 0, :], True, False)
                    ins = mm(ps[:, P + h * HD:P + (h + 1) * HD], dT[:, 2 * P:3 * P], vh[:, 1, :], False, True)
                ins.then_inc(done, 1)

            def turn_output(j):
                emptied(pe, sums, f"pv{j}")
                ps, done = begin(pe, sums, f"oT{j}")
                for t in range(TT):
                    ins = nc.tensor.transpose(ps[:, t * P:(t + 1) * P], osc[:, j % 2, t, :], ident)
                ins.then_inc(done, 1)

            def unit(s):
                if not s2:
                    return
                if s < UNITS:
                    scores(s)
                if 1 <= s <= UNITS:
                    turn_difference(s - 1)
                if 3 <= s:
                    turn_output(s - 3)
                if 2 <= s < UNITS + 2:
                    weigh(s - 2)

            def output(t):
                product(f"wo{t}", [[(oT[:, j, t * P:(t + 1) * P], wo_sb[:, j, :]) for j in range(UNITS)]])

            def qkv(t, part):
                if rd.first(1) and t == 0:
                    pe.wait_ge(wqkv_in[part], 16)
                product(("qa", "qb", "kv")[part] + str(t),
                        [[(xnT[:, c, t * P:(t + 1) * P], wqkv_sb[:, c, part * BANK:(part + 1) * BANK]) for c in range(KC)]])

            def context_v(n):
                product(f"vx{n}", [[(ct[:, t, lt * P:(lt + 1) * P], wx_sb[:, 2, t, :]) for t in range(TT)]
                                   for lt in (2 * n, 2 * n + 1)], T)

            def turn_weights(q):
                pe.wait_ge(xnorm, (r - 1) * 4 + (q + 1))
                turn(f"pT{q}", [pr[:, q, k * P:(k + 1) * P] for k in range(4)])

            def mixed(n):
                product(f"h{n}", [[(vx[:, k, n * P:(n + 1) * P], prT[:, k, :]) for k in range(4)]])

            def turn_queries(n):
                turn(f"qT{n}", [qk[:, t, j * P:(j + 1) * P] for j in (2 * n, 2 * n + 1) for t in range(TT)])

            def context_k(n):
                product(f"kx{n}", [[(wx_sb[:, 1, t, n * P:(n + 1) * P], ct[:, t, :]) for t in range(TT)]])

            unit(0)
            if s3:
                context_k(1)
                pe.wait_ge(gdone, r)
                output(0)
            unit(1)
            if s3:
                output(1)
            unit(2)
            if s3:
                context_v(0)
            if s1:
                pe.wait_ge(normed[0], (r + 2) * TT)
                for n in range(2):
                    turn(f"xnT{n}", [xn[:, t, c * P:(c + 1) * P] for c in (2 * n, 2 * n + 1) for t in range(TT)])
            unit(3)
            if s1:
                emptied(pe, turns, "xnT0")
                emptied(pe, turns, "xnT1")
                qkv(0, 0)
            if s4:
                pe.wait_ge(normed[1], (r - 1) * (2 * TT))
                for n in range(2):
                    turn(f"rT{n}", [row[:, t, c * P:(c + 1) * P] for c in (2 * n, 2 * n + 1) for t in range(TT)])
            if s1:
                qkv(0, 1)
            unit(4)
            if s3:
                pe.wait_ge(normed[1], (r - 1) * (2 * TT) + TT)
                for n in range(2):
                    product(f"qx{n}", [[(wx_sb[:, 0, t, n * P:(n + 1) * P], xn2[:, t, :]) for t in range(TT)]])
            if s4:
                emptied(pe, turns, "rT0")
                emptied(pe, turns, "rT1")
                for t in range(TT):
                    product(f"route{t}", [[(rT[:, c, t * P:(t + 1) * P], wr_sb[:, c, :]) for c in range(KC)]], EXPERTS)
            unit(5)
            if s3:
                for name in ("kx1", "qx0", "qx1"):
                    emptied(pe, sums, name)
                for q in range(4):
                    ps, done = begin(pe, score, f"x{q}")
                    mm(ps, qx[:, 0, q * P:(q + 1) * P], kx[:, 0, :], True, False)
                    mm(ps, qx[:, 1, q * P:(q + 1) * P], kx[:, 1, :], False, True).then_inc(done, 1)
            if s1:
                qkv(0, 2)
                qkv(1, 0)
            unit(6)
            if s3:
                context_v(1)
            unit(7)
            if s3:
                turn_weights(0)
                turn_weights(1)
            if s1:
                qkv(1, 1)
            if s3:
                turn_weights(2)
                turn_weights(3)
            unit(8)
            if s1:
                qkv(1, 2)
            if s4:
                pe.wait_ge(row_in, r - 1)
                turn("keyT", [keyed[:, :, :].rearrange("p a b -> p (a b)")])
            if s3:
                emptied(pe, turns, "pT2")
                emptied(pe, turns, "pT3")
                emptied(pe, sums, "vx0")
                emptied(pe, sums, "vx1")
                mixed(0)
            if s1:
                pe.wait_ge(rope_sum, (r + 2) * (3 * TT))
                turn("kT", [qk[:, t, (UNITS + g) * P:(UNITS + g + 1) * P] for g in range(2) for t in range(TT)])
            if s3:
                mixed(1)
            if s1:
                turn_queries(0)
                turn_queries(1)
            unit(9)
            unit(10)
            if s1:
                turn_queries(2)
                turn_queries(3)
            if s2:
                heads = tab[:, HEADS:HEADS + P]
                pe.wait_ge(gstat, r + 1)
                product("gmean", [[(heads, gmv[:, :, 0])]], UNITS)
                if rd.first(2):
                    pe.wait_ge(later_in, 16 * 3)
                pe.wait_ge(ctx_in, r * 16 + 16)
                context_k(0)
                emptied(pe, sums, "gmean")
                product("gvar", [[(heads, gdev[:, :])]], UNITS)
            if s1:
                emptied(pe, turns, "qT2")
                emptied(pe, turns, "qT3")
            for ring in (score, turns, sums):
                ring.ended()

        rounds(nc.tensor.Fori, body)

    block_context.__exit__(None, None, None)


def experts(nc, st, psum, w13, w2, out, table, keys, tab):
    def sb(name, shape, dt=FP32):
        return st.enter_context(nc.sbuf_tensor(name, shape, dt))

    def sem(name):
        return st.enter_context(nc.semaphore(name))

    def pairs(fori, pair):
        for n in range(SLOTS):
            pair(n, 0, n)
        with fori(1, PAIRS // SLOTS - 2) as i:
            for n in range(SLOTS):
                pair(i * SLOTS + n, i, n)
        for k in range(PAIRS - 2 * SLOTS, PAIRS):
            pair(k, k // SLOTS, k % SLOTS, PAIRS - k)

    SLOTS = 4
    w13_sb = [sb(f"w13_sb{n}", [P, 2, KC * 2 * FF]) for n in range(SLOTS)]
    w2a_sb = [sb(f"w2a_sb{n}", [P, 2, D]) for n in range(SLOTS)]
    w2b_sb = [sb(f"w2b_sb{n}", [FF - P, 2, D]) for n in range(SLOTS)]
    ident = tab[:, IDENT:IDENT + P]
    firsts = sb("firsts", [P, CAP])
    both = sb("both", [EXPERTS, 2 * CAP])
    slot = sb("slot", [EXPERTS, CAP])
    sloti, low, high = (sb(n, [EXPERTS, CAP], I32) for n in ("sloti", "low", "high"))
    held = sb("held", [EXPERTS, CAP])
    rowf = sb("rowf", [EXPERTS, 2, CAP])
    tmp, rows_to = sb("tmp", [EXPERTS, CAP]), sb("rows_to", [EXPERTS, CAP])
    from_idx = sb("from_idx", [P, PAIRS], I32)
    to_idx = sb("to_idx", [CAP, EXPERTS], I32)
    gidx = [sb(f"gidx{n}", [P, 1], I32) for n in range(SLOTS)]
    sidx = [sb(f"sidx{n}", [CAP, 1], I32) for n in range(2)]
    gx = [sb(f"gx{n}", [P, ROW]) for n in range(SLOTS)]
    wcol = [sb(f"wcol{n}", [P, 1]) for n in range(SLOTS)]
    gxT = [sb(f"gxT{n}", [P, KC, P]) for n in range(2)]
    eh = [sb(f"eh{n}", [P, FF]) for n in range(2)]
    sig, gate = ([sb(f"{name}{n}", [P, FF]) for n in range(2)] for name in ("sig", "gate"))
    g = [sb(f"g{n}", [P, FF]) for n in range(2)]
    gT = [sb(f"gT{n}", [P, 2, P]) for n in range(2)]
    y = [sb(f"y{n}", [P, D]) for n in range(SLOTS)]
    zeros = sb("zeros", [CAP, D])

    pick, joined = sem("pick"), sem("joined")
    picked_out, rows_in, index_in = sem("picked_out"), sem("rows_in"), sem("index_in")
    zero_in, zero_out = sem("zero_in"), sem("zero_out")
    w_in = [sem(f"w_in{n}") for n in range(SLOTS)]
    idx_in, sidx_in, added = sem("idx_in"), sem("sidx_in"), sem("added")
    gx_in = [sem(f"gx_in{n}") for n in range(SLOTS)]
    gx_turned, gxT_in, wcol_in = sem("gx_turned"), sem("gxT_in"), sem("wcol_in")
    hidden, eh_in, g_in, g_turned, gT_in, y_full, y_in = (
        sem(n) for n in ("hidden", "eh_in", "g_in", "g_turned", "gT_in", "y_full", "y_in"))
    moe_step = sem("moe_step")

    turn_ps = [psum[:, n, :] for n in range(2)]
    hidden_ps = [psum[:, 2 + n, 0:2 * FF] for n in range(2)]
    gate_ps = [psum[:, 4 + n, 0:2 * P] for n in range(2)]
    y_ps = [psum[:, 6 + n, :] for n in range(2)]

    with nc.Block() as block:
        @block.sync
        def _(sp):
            def first_weights(k, n):
                sp.dma_start(w13_sb[n][:, :, :], w13[bass.ds(2 * k, 2)].rearrange("h p f -> p h f")).then_inc(w_in[n], 16)

            def second_weights(k, n):
                for dst, lo, hi in ((w2a_sb[n], 0, P), (w2b_sb[n], P, FF)):
                    sp.dma_start(dst[:, :, :], w2[bass.ds(2 * k, 2), lo:hi, :].rearrange("h p f -> p h f")).then_inc(w_in[n], 16)

            first_weights(0, 0)
            second_weights(0, 0)
            sp.wait_ge(zero_in, 1)
            sp.dma_start(out[TOKENS:TOKENS + CAP, :], zeros[:, :]).then_inc(zero_out, 16)
            sp.wait_ge(pick, 8)
            sp.dma_start(both[:, 0:CAP], firsts[0:EXPERTS, :]).then_inc(joined, 16)
            sp.dma_start(both[:, CAP:2 * CAP], firsts[EXPERTS:P, :]).then_inc(joined, 16)
            for n in range(1, SLOTS):
                if n == 2:
                    sp.wait_ge(idx_in, SLOTS)
                first_weights(n, n)
                second_weights(n, n)
            with nc.sync.Fori(0, PAIRS // SLOTS - 1) as i:
                for n in range(SLOTS):
                    sp.wait_ge(hidden, i * SLOTS + (n + 1))
                    alone(sp)
                    first_weights(i * SLOTS + (SLOTS + n), n)
                    sp.wait_ge(y_full, i * SLOTS + (n + 1))
                    alone(sp)
                    second_weights(i * SLOTS + (SLOTS + n), n)

        @block.gpsimd
        def _(pool):
            nc.gpsimd.memset(zeros[:, :], 0.0).then_inc(zero_in, 1)
            pool.wait_ge(zero_out, 16)
            pool.wait_ge(index_in, 2)

            def fetch(k, n):
                nc.gpsimd.tensor_copy(gidx[n][:, :], from_idx[:, bass.ds(k, 1)]).then_inc(idx_in, 1)
                pool.wait_ge(idx_in, k + 1)
                alone(pool)
                nc.gpsimd.indirect_dma_start(
                    out=gx[n][:, :], out_offset=None, in_=table,
                    in_offset=bass.IndirectOffsetOnAxis(ap=gidx[n][:, 0:1], axis=0)).then_inc(gx_in[n], 16)

            def to_rows(k, h):
                nc.gpsimd.tensor_copy(sidx[h][:, :], to_idx[:, bass.ds(2 * k + h, 1)]).then_inc(sidx_in, 1)

            def add(k, n, h):
                pool.wait_ge(sidx_in, 2 * k + (h + 1))
                if h or not isinstance(k, int) or k:
                    pool.wait_ge(added, k * 32 + 16 * h)
                alone(pool)
                nc.gpsimd.indirect_dma_start(
                    out=out, out_offset=bass.IndirectOffsetOnAxis(ap=sidx[h][:, 0:1], axis=0),
                    in_=y[n][h * CAP:(h + 1) * CAP, :], in_offset=None, compute_op=ALU.add).then_inc(added, 16)

            def pair(k, i, n, left=PAIRS):
                to_rows(k, 0)
                pool.wait_ge(y_in, k + 1)
                add(k, n, 0)
                to_rows(k, 1)
                if left > SLOTS + 1:
                    fetch(k + (SLOTS + 1), (n + 1) % SLOTS)
                add(k, n, 1)

            for n in range(SLOTS):
                fetch(n, n)
            pool.wait_ge(gx_turned, 1)
            pool.wait_ge(wcol_in, 1)
            fetch(SLOTS, 0)
            pairs(nc.gpsimd.Fori, pair)
            pool.wait_ge(added, PAIRS * 32)

        @block.scalar
        def _(act):
            def tokens(k, n):
                act.wait_ge(gx_turned, k + 1)
                nc.scalar.copy(gxT[n % 2][:, :, :], turn_ps[n % 2].rearrange("p (c s) -> p c s", c=KC)).then_inc(gxT_in, 1)

            def exponential(k, n):
                act.wait_ge(hidden, k + 1)
                nc.scalar.activation(eh[n % 2][:, :], hidden_ps[n % 2][:, 0:FF], ACT.Exp, scale=-1.0).then_inc(eh_in, 1)

            def gated(k, n):
                act.wait_ge(g_turned, k + 1)
                nc.scalar.copy(gT[n % 2][:, 0, :], gate_ps[n % 2][:, 0:P])
                nc.scalar.copy(gT[n % 2][0:FF - P, 1, :], gate_ps[n % 2][0:FF - P, P:2 * P]).then_inc(gT_in, 1)

            tokens(0, 0)
            exponential(0, 0)
            tokens(1, 1)

            def pair(k, i, n, left=PAIRS):
                if left > 1:
                    exponential(k + 1, n + 1)
                gated(k, n)
                if left > 2:
                    tokens(k + 2, n + 2)

            pairs(nc.scalar.Fori, pair)

        @block.vector
        def _(dve):
            vec = nc.vector

            rounds = CAP // 8

            def earliest(src, dst, call):
                for r in range(rounds):
                    vec.max(dst[:, 8 * r:8 * r + 8], src).then_inc(pick, 1)
                    dve.wait_ge(pick, call * rounds + r + 1)
                    if r < rounds - 1:
                        vec.match_replace(src, dst[:, 8 * r:8 * r + 8], src, 0.0).then_inc(picked_out, 1)
                        dve.wait_ge(picked_out, call * (rounds - 1) + r + 1)

            earliest(keys[:, LATE * P - CAP:], firsts[:, :], 0)
            dve.wait_ge(joined, 32)
            earliest(both[:, :], slot[:, :], 1)
            done = [0]

            def then(ins):
                done[0] += 1
                ins.then_inc(rows_in, 1)
                dve.wait_ge(rows_in, done[0])

            then(vec.tensor_scalar(sloti[:, :], slot[:, :], -1.0, float(TOKENS), ALU.mult, ALU.add))
            then(vec.tensor_scalar(low[:, :], sloti[:, :], B - 1, 8, ALU.bitwise_and, ALU.logical_shift_left))
            then(vec.tensor_scalar(high[:, :], sloti[:, :], 4, T - 1, ALU.logical_shift_right, ALU.bitwise_and))
            then(vec.tensor_tensor(tmp[:, :], low[:, :], high[:, :], ALU.add))
            then(vec.tensor_scalar(held[:, :], slot[:, :], 0.5, None, ALU.is_gt))
            then(vec.tensor_tensor(rowf[:, 0, :], tmp[:, :], held[:, :], ALU.mult))
            then(vec.tensor_copy(rowf[:, 1, :], rowf[:, 0, :]))
            then(vec.tensor_tensor(tmp[:, :], tab[0:EXPERTS, SPARE:SPARE + CAP], held[:, :], ALU.mult))
            then(vec.tensor_tensor(tmp[:, :], tab[0:EXPERTS, SPARE:SPARE + CAP], tmp[:, :], ALU.subtract))
            then(vec.tensor_tensor(rows_to[:, :], tmp[:, :], rowf[:, 0, :], ALU.add))
            dve.wait_ge(index_in, 1)
            dup = turn_ps[0][:, 0:EXPERTS].rearrange("p (k e) -> p k e", e=2)
            vec.tensor_copy(from_idx[0:CAP, :], dup[0:CAP, :, 0])
            vec.tensor_copy(from_idx[CAP:P, :], dup[CAP:P, :, 1])
            vec.tensor_copy(to_idx[:, :], turn_ps[1][0:CAP, 0:EXPERTS]).then_inc(index_in, 1)

            def silu(k, i, n):
                m = n % SLOTS
                dve.wait_ge(gx_in[m], i * 16 + (n // SLOTS * 16 + 16))
                alone(dve)
                vec.tensor_copy(wcol[m][0:CAP, :], gx[m][0:CAP, bass.ds(D + 2 * k, 1)])
                vec.tensor_copy(wcol[m][CAP:P, :], gx[m][CAP:P, bass.ds(D + 1 + 2 * k, 1)]).then_inc(wcol_in, 1)
                dve.wait_ge(eh_in, k + 1)
                alone(dve)
                vec.tensor_scalar(sig[n % 2][:, :], eh[n % 2][:, :], 1.0, None, ALU.add).then_inc(moe_step, 1)
                dve.wait_ge(moe_step, 3 * k + 1)
                vec.reciprocal(gate[n % 2][:, :], sig[n % 2][:, :]).then_inc(moe_step, 1)
                dve.wait_ge(moe_step, 3 * k + 2)
                vec.tensor_tensor(sig[n % 2][:, :], hidden_ps[n % 2][:, 0:FF], gate[n % 2][:, :], ALU.mult).then_inc(moe_step, 1)
                dve.wait_ge(moe_step, 3 * k + 3)
                vec.tensor_tensor(g[n % 2][:, :], hidden_ps[n % 2][:, FF:2 * FF], sig[n % 2][:, :], ALU.mult).then_inc(g_in, 1)

            silu(0, 0, 0)

            def pair(k, i, n, left=PAIRS):
                if left > 1:
                    silu(k + 1, i, n + 1)
                dve.wait_ge(wcol_in, k + 1)
                if not isinstance(k, int) or k >= SLOTS:
                    dve.wait_ge(added, k * 32 - (SLOTS - 1) * 32)
                dve.wait_ge(y_full, k + 1)
                vec.tensor_scalar(y[n][:, :], y_ps[n % 2], wcol[n][:, 0:1], None, ALU.mult).then_inc(y_in, 1)

            pairs(nc.vector.Fori, pair)

        @block.tensor
        def _(pe):
            mm = nc.tensor.matmul
            pe.wait_ge(rows_in, 10)
            nc.tensor.transpose(turn_ps[0][:, 0:EXPERTS], rowf[:, :, :].rearrange("e a s -> e (a s)"), ident[0:EXPERTS, 0:EXPERTS])
            nc.tensor.transpose(turn_ps[1][0:CAP, 0:EXPERTS], rows_to[:, :], ident[0:EXPERTS, 0:EXPERTS]).then_inc(index_in, 1)
            pe.wait_ge(index_in, 2)

            def turn_tokens(k, i, n):
                m = n % SLOTS
                pe.wait_ge(gx_in[m], i * 16 + (n // SLOTS * 16 + 16))
                for c in range(KC):
                    ins = nc.tensor.transpose(turn_ps[n % 2][:, c * P:(c + 1) * P], gx[m][:, c * P:(c + 1) * P], ident)
                ins.then_inc(gx_turned, 1)

            def hidden_layer(k, i, n):
                m = n % SLOTS
                pe.wait_ge(gxT_in, k + 1)
                pe.wait_ge(w_in[m], i * 48 + (n // SLOTS * 48 + 48))
                alone(pe)
                for c in range(KC):
                    for h in range(2):
                        s = slice(h * CAP, (h + 1) * CAP)
                        ins = mm(hidden_ps[n % 2][s, :], gxT[n % 2][:, c, s], w13_sb[m][:, h, c * 2 * FF:(c + 1) * 2 * FF],
                                 start=(c == 0), stop=(c == KC - 1), skip_group_check=True)
                ins.then_inc(hidden, 1)

            def turn_gated(k, n):
                pe.wait_ge(g_in, k + 1)
                nc.tensor.transpose(gate_ps[n % 2][:, 0:P], g[n % 2][:, 0:P], ident)
                nc.tensor.transpose(gate_ps[n % 2][0:FF - P, P:2 * P], g[n % 2][:, P:FF], ident).then_inc(g_turned, 1)

            def output_layer(k, n):
                pe.wait_ge(gT_in, k + 1)
                alone(pe)
                for lo, w in ((0, w2a_sb), (P, w2b_sb)):
                    rows = P if lo == 0 else FF - P
                    for h in range(2):
                        s = slice(h * CAP, (h + 1) * CAP)
                        ins = mm(y_ps[n % 2][s, :], gT[n % 2][0:rows, lo // P, s], w[n][:, h, :],
                                 start=(lo == 0), stop=(lo > 0), skip_group_check=True)
                ins.then_inc(y_full, 1)

            turn_tokens(0, 0, 0)
            hidden_layer(0, 0, 0)
            turn_tokens(1, 0, 1)

            def pair(k, i, n, left=PAIRS):
                if left > 1:
                    hidden_layer(k + 1, i, n + 1)
                turn_gated(k, n)
                if left > 2:
                    turn_tokens(k + 2, i, n + 2)
                output_layer(k, n)

            pairs(nc.tensor.Fori, pair)


def constants():
    tabs = np.zeros((P, TAB), np.float32)
    tabs[:, IDENT:IDENT + P] = np.eye(P)
    tri = np.where(np.arange(P)[None, :] > np.arange(P)[:, None], MASKED, 0.0)
    tabs[:, TRI:TRI + 4 * P] = np.tile(tri, (1, 4))
    tabs[:, HEADS:HEADS + P] = np.kron(np.eye(P // HD), np.full((HD, HD), 1.0 / HD))
    inv = (1.0 / np.float32(10000.0) ** (np.arange(0, DH, 2, dtype=np.float32) / np.float32(DH))).astype(np.float32)
    angle = (np.arange(T, dtype=np.float32)[:, None] * inv[None, :]).astype(np.float32).astype(np.float64)
    for t in range(TT):
        a = angle[t * P:(t + 1) * P]
        tabs[:, COS + t * DH:COS + (t + 1) * DH] = np.concatenate([np.cos(a), np.cos(a)], 1)
        tabs[:, SIN + t * DH:SIN + (t + 1) * DH] = np.concatenate([-np.sin(a), np.sin(a)], 1)
        tabs[:, KEY0 + t] = TOKENS - B * (t * P + np.arange(P))
    tabs[:, SPARE:SPARE + CAP] = TOKENS + np.arange(CAP)
    return tabs


def chunks(w):
    return np.ascontiguousarray(w.reshape(-1, P, w.shape[-1]).transpose(1, 0, 2))


def kernel(x, ctx_2048, L0_attn_Wq, L0_attn_Wk, L0_attn_Wv, L0_attn_Wo, L0_attn_lambda_q1, L0_attn_lambda_k1,
           L0_attn_lambda_q2, L0_attn_lambda_k2, L0_attn_gn_w, L0_attn_gn_b, L0_xattn_QW, L0_xattn_Qb, L0_xattn_KW,
           L0_xattn_Kb, L0_xattn_VW, L0_xattn_Vb, L0_ffn_router_w, L0_ffn_w1, L0_ffn_v1, L0_ffn_w2):
    import concourse.bacc as bacc
    from concourse.bass_utils import run_bass_kernel_spmd

    heads = np.array([[4 * (2 * (j // 4) + h) + j % 4 for h in range(2)] for j in range(UNITS)]).reshape(-1)
    pairs = np.concatenate([np.arange(0, DH, 2), np.arange(1, DH, 2)])
    inner = np.concatenate([i * DH + pairs for i in range(2)])
    q_cols = (heads[:, None] * HD + inner[None, :]).reshape(-1)
    k_cols = (np.arange(KV)[:, None] * HD + inner[None, :]).reshape(-1)
    o_rows = (heads[:, None] * HD + np.arange(HD)[None, :]).reshape(-1)
    a = {k: np.asarray(w) for k, w in locals().items() if k.startswith("L0_")}

    def columns(v):
        return v.reshape(-1, P).T

    lams = np.concatenate([a[f"L0_attn_lambda_{n}"] for n in ("q1", "k1", "q2", "k2")])
    cols = np.concatenate([columns(a["L0_attn_gn_w"][o_rows]), columns(a["L0_attn_gn_b"][o_rows]),
                           columns(a["L0_xattn_Qb"]), columns(a["L0_xattn_Kb"]), columns(a["L0_xattn_Vb"]),
                           np.broadcast_to(lams, (P, 4 * DH))], axis=1)
    w13 = np.concatenate([a["L0_ffn_w1"], a["L0_ffn_v1"]], axis=1)
    w13 = w13.transpose(0, 2, 1).reshape(EXPERTS, KC, P, 2 * FF).transpose(0, 2, 1, 3)
    arrays = {
        "x": np.asarray(x).reshape(TOKENS, D),
        "ctx": np.asarray(ctx_2048).reshape(TOKENS, D),
        "wqkv": chunks(np.concatenate([a["L0_attn_Wq"][:, q_cols], a["L0_attn_Wk"][:, k_cols], a["L0_attn_Wv"]], 1)),
        "wo": chunks(a["L0_attn_Wo"][o_rows]),
        "wx": np.stack([chunks(a[f"L0_xattn_{n}W"].T) for n in "QKV"], 1),
        "wr": chunks(a["L0_ffn_router_w"].T),
        "cols": cols,
        "tabs": constants(),
        "w13": w13.reshape(EXPERTS, P, KC * 2 * FF),
        "w2": a["L0_ffn_w2"].reshape(EXPERTS, FF, D),
    }
    arrays = {k: np.ascontiguousarray(v) for k, v in arrays.items()}
    nc = bacc.Bacc("TRN2", target_bir_lowering=False, num_devices=1)
    args = [nc.dram_tensor(k, v.shape, FP32, kind="ExternalInput").ap() for k, v in arrays.items()]
    out = nc.dram_tensor("out", (TOKENS + CAP, D), FP32, kind="ExternalOutput").ap()
    table = nc.dram_tensor("table", (TOKENS, ROW), FP32, kind="Internal").ap()
    build(nc, *args, out, table)
    r = run_bass_kernel_spmd(nc, [arrays], core_ids=[0])
    return r.results[0]["out"][:TOKENS].reshape(B, T, D)
```
